# Optimizing a Trainium2 kernel written in Bass

```python
import numpy as np
import jax
import jax.numpy as jnp

def _softmax(x, axis=-1):
    return jax.nn.softmax(x, axis=axis)

def _gelu(x):
    return jax.nn.gelu(x, approximate=True)

def _silu(x):
    return jax.nn.silu(x)

def _sigmoid(x):
    return jax.nn.sigmoid(x)

def _layernorm(x, axis=-1, eps=1e-05):
    m = jnp.mean(x, axis=axis, keepdims=True)
    v = jnp.var(x, axis=axis, keepdims=True)
    return (x - m) / jnp.sqrt(v + eps)

def _scatter_add(tgt, idx, src, axis=0):
    return tgt.at[idx].add(src)

def _segment_sum(src, seg, n):
    return jax.ops.segment_sum(src, seg, n)
kernel_name = 'mk_flamingo_gated_d1_seqx_r2_9fb81b'

def setup_inputs(seed: int=0):
    np.random.seed(seed)
    _w = jnp.asarray

    def _rec_inputs():
        import jax
        import jax.numpy as jnp
        _rk = jax.random.key(seed)
        x = 0.5 + 0.2887 * jax.random.normal(jax.random.fold_in(_rk, 1), (4, 1024, 1024), jnp.float32)
        _lenS = 1024 - jax.random.randint(jax.random.fold_in(_rk, 7), (4,), 0, max(1, 1024 // 4) + 1, jnp.int32)
        _lenS2 = 1024 - jax.random.randint(jax.random.fold_in(_rk, 8), (4,), 0, max(1, 1024 // 4) + 1, jnp.int32)
        _ctx_512P = jax.random.normal(jax.random.fold_in(_rk, 11), (4, 16, 256), jnp.float32)
        _ctx_512c = jax.random.dirichlet(jax.random.fold_in(_rk, 511), 0.3 * jnp.ones((16,), jnp.float32), (4, 1024))
        _ctx_512t = jnp.einsum('bsk,bkd->bsd', _ctx_512c, _ctx_512P)
        _ctx_512t = _ctx_512t * jax.lax.rsqrt(jnp.mean(jnp.square(_ctx_512t)) + 1e-12) * 0.953939
        ctx_512 = 7.22013e-05 + 1.00017 * (_ctx_512t + 0.3 * jax.random.normal(jax.random.fold_in(_rk, 611), (4, 1024, 256), jnp.float32))
        _validS = jnp.arange(1024)[None, :] < _lenS[:, None]
        _validS2 = jnp.arange(1024)[None, :] < _lenS2[:, None]
        _causal = jnp.tril(jnp.ones((1024, 1024), dtype=bool))
        mask_SxS2_bk1 = jnp.broadcast_to(_validS2[0:1, :], (1024, 1024))
        mask_BxS2_bf0 = jnp.logical_not(jnp.ones((4, 1024), dtype=bool))
        _g = jax.random.normal(jax.random.fold_in(_rk, 9001), (2, 1), jnp.float32)
        _g = jnp.sign(_g) * jnp.maximum(jnp.abs(_g), 1.0) + (_g == 0) * 1.0
        g_xattn = _g[0]
        g_ffn = _g[1]
        return (x, ctx_512, mask_SxS2_bk1, mask_BxS2_bf0, g_xattn, g_ffn)
    x, ctx_512, mask_SxS2_bk1, mask_BxS2_bf0, g_xattn, g_ffn = _rec_inputs()

    def _L0_xattn_setup():
        import jax, jax.numpy as jnp
        import numpy as np
        B, S, H = (8, 1024, 256)
        key = jax.random.key(seed)
        kq, kk, kqc, kwq, kwk = jax.random.split(key, 5)
        q = jax.random.normal(kq, (B, S, H), dtype=jnp.float32)
        k = jax.random.normal(kk, (B, S, H), dtype=jnp.float32)
        qc_score = jax.random.uniform(kqc, (B, S, S), dtype=jnp.float32)
        attn_mask = jnp.triu(jnp.ones((S, S), dtype=bool), k=1)
        key_padding_mask = jnp.zeros((B, S), dtype=bool)
        scale = 1.0 / np.sqrt(H)
        Wq = jax.random.normal(kwq, (H, H), dtype=jnp.float32) * scale
        Wk = jax.random.normal(kwk, (H, H), dtype=jnp.float32) * scale
        bq = jnp.zeros((H,), dtype=jnp.float32)
        bk = jnp.zeros((H,), dtype=jnp.float32)
        return {'q': q, 'k': k, 'attn_mask': attn_mask, 'key_padding_mask': key_padding_mask, 'qc_score': qc_score, 'Wq': Wq, 'bq': bq, 'Wk': Wk, 'bk': bk}
    _L0_xattn_all = _L0_xattn_setup()
    _L0_xattn_in = {k: v for k, v in _L0_xattn_all.items() if k in ('Wq', 'bq', 'Wk', 'bk')}
    del _L0_xattn_all

    def _L0_ffn_setup():
        import jax, jax.numpy as jnp
        import numpy as np
        E = 64
        K = 8
        H = 1024
        I = 384
        CAP = 256

        def _moe(hidden_states, gate_w, wg, wu, wd):
            B, S, Hd = hidden_states.shape
            x = hidden_states.reshape(-1, Hd)
            T = x.shape[0]
            logits = x @ gate_w.T
            probs = jax.nn.softmax(logits.astype(jnp.float32), axis=-1)
            w, sel = jax.lax.top_k(probs, K)
            w = w / jnp.sum(w, axis=-1, keepdims=True)
            w = w.astype(x.dtype)
            eid = sel.reshape(-1)
            tok = jnp.repeat(jnp.arange(T), K)
            oh = jax.nn.one_hot(eid, E, dtype=jnp.int32)
            pos = jnp.sum(jnp.cumsum(oh, axis=0) * oh, axis=-1) - 1
            valid = pos < CAP
            slot = jnp.where(valid, pos, CAP)
            xin = jnp.zeros((E, CAP + 1, Hd), x.dtype).at[eid, slot].set(x[tok])
            inp = xin[:, :CAP]
            h = jax.nn.silu(jnp.einsum('ech,ehi->eci', inp, wg)) * jnp.einsum('ech,ehi->eci', inp, wu)
            out = jnp.einsum('eci,eih->ech', h, wd)
            out_pad = jnp.concatenate([out, jnp.zeros((E, 1, Hd), out.dtype)], axis=1)
            g = out_pad[eid, slot] * (w.reshape(-1) * valid.astype(w.dtype))[:, None]
            y = jnp.zeros((T, Hd), x.dtype).at[tok].add(g)
            return y.reshape(B, S, Hd)
        key = jax.random.key(seed)
        k1, k2, k3, k4, k5 = jax.random.split(key, 5)
        hidden_states = jax.random.normal(k1, (1, 1024, H), dtype=jnp.float32)
        gate_w = jax.random.normal(k2, (E, H), dtype=jnp.float32) * 0.02
        wg = jax.random.normal(k3, (E, H, I), dtype=jnp.float32) * 0.02
        wu = jax.random.normal(k4, (E, H, I), dtype=jnp.float32) * 0.02
        wd = jax.random.normal(k5, (E, I, H), dtype=jnp.float32) * 0.02
        return {'hidden_states': hidden_states, 'gate_w': gate_w, 'wg': wg, 'wu': wu, 'wd': wd}
    _L0_ffn_all = _L0_ffn_setup()
    _L0_ffn_in = {k: v for k, v in _L0_ffn_all.items() if k in ('gate_w', 'wg', 'wu', 'wd')}
    del _L0_ffn_all
    return {'x': x, 'ctx_512': ctx_512, 'mask_SxS2_bk1': mask_SxS2_bk1, 'mask_BxS2_bf0': mask_BxS2_bf0, 'g_xattn': g_xattn, 'g_ffn': g_ffn, 'L0_xattn_Wq': _L0_xattn_in['Wq'], 'L0_xattn_bq': _L0_xattn_in['bq'], 'L0_xattn_Wk': _L0_xattn_in['Wk'], 'L0_xattn_bk': _L0_xattn_in['bk'], 'L0_ffn_gate_w': _L0_ffn_in['gate_w'], 'L0_ffn_wg': _L0_ffn_in['wg'], 'L0_ffn_wu': _L0_ffn_in['wu'], 'L0_ffn_wd': _L0_ffn_in['wd']}

def reference(x, ctx_512, mask_SxS2_bk1, mask_BxS2_bf0, g_xattn, g_ffn, L0_xattn_Wq, L0_xattn_bq, L0_xattn_Wk, L0_xattn_bk, L0_ffn_gate_w, L0_ffn_wg, L0_ffn_wu, L0_ffn_wd):
    import jax
    import jax.numpy as jnp

    def _L0_xattn_ref(q, k, attn_mask, key_padding_mask, qc_score, Wq, bq, Wk, bk):
        import jax, jax.numpy as jnp
        import numpy as np
        B, S, H = (8, 1024, 256)
        qp = jnp.einsum('bsh,oh->bso', q, Wq) + bq
        kp = jnp.einsum('bth,oh->bto', k, Wk) + bk
        scaling = jnp.asarray(float(H) ** (-0.5), dtype=qp.dtype)
        scores = jnp.einsum('bsh,bth->bst', qp, kp) * scaling
        scores = scores * qc_score
        mask = attn_mask[None, :, :] | key_padding_mask[:, None, :]
        scores = jnp.where(mask, -jnp.inf, scores)
        return jax.nn.softmax(scores, axis=-1)

    def _L0_ffn_ref(hidden_states, gate_w, wg, wu, wd):
        import jax, jax.numpy as jnp
        import numpy as np
        E = 64
        K = 8
        H = 1024
        I = 384
        CAP = 256

        def _moe(hidden_states, gate_w, wg, wu, wd):
            B, S, Hd = hidden_states.shape
            x = hidden_states.reshape(-1, Hd)
            T = x.shape[0]
            logits = x @ gate_w.T
            probs = jax.nn.softmax(logits.astype(jnp.float32), axis=-1)
            w, sel = jax.lax.top_k(probs, K)
            w = w / jnp.sum(w, axis=-1, keepdims=True)
            w = w.astype(x.dtype)
            eid = sel.reshape(-1)
            tok = jnp.repeat(jnp.arange(T), K)
            oh = jax.nn.one_hot(eid, E, dtype=jnp.int32)
            pos = jnp.sum(jnp.cumsum(oh, axis=0) * oh, axis=-1) - 1
            valid = pos < CAP
            slot = jnp.where(valid, pos, CAP)
            xin = jnp.zeros((E, CAP + 1, Hd), x.dtype).at[eid, slot].set(x[tok])
            inp = xin[:, :CAP]
            h = jax.nn.silu(jnp.einsum('ech,ehi->eci', inp, wg)) * jnp.einsum('ech,ehi->eci', inp, wu)
            out = jnp.einsum('eci,eih->ech', h, wd)
            out_pad = jnp.concatenate([out, jnp.zeros((E, 1, Hd), out.dtype)], axis=1)
            g = out_pad[eid, slot] * (w.reshape(-1) * valid.astype(w.dtype))[:, None]
            y = jnp.zeros((T, Hd), x.dtype).at[tok].add(g)
            return y.reshape(B, S, Hd)
        return _moe(hidden_states, gate_w, wg, wu, wd)
    x = x + jnp.tanh(g_xattn[0]) * _L0_xattn_ref(ctx_512, ctx_512, mask_SxS2_bk1, mask_BxS2_bf0, _layernorm(x, axis=-1), L0_xattn_Wq, L0_xattn_bq, L0_xattn_Wk, L0_xattn_bk)
    x = x + jnp.tanh(g_ffn[0]) * _L0_ffn_ref(_layernorm(x, axis=-1), L0_ffn_gate_w, L0_ffn_wg, L0_ffn_wu, L0_ffn_wd)
    return x

_drawn_inputs = setup_inputs


def setup_inputs(seed=0):
    import zlib

    import numpy as np

    out = dict(_drawn_inputs(seed))
    spreads = {'L0_xattn_bq': (0.0, 0.8), 'L0_xattn_bk': (0.0, 0.8)}
    factors = {'ctx_512': 4.484, 'L0_xattn_Wq': 4.432, 'L0_xattn_Wk': 4.484}
    for name, (base, spread) in spreads.items():
        noise = np.random.default_rng([zlib.crc32(name.encode()), seed]).standard_normal(out[name].shape)
        drawn = base * np.exp(spread * noise) if base else spread * noise
        out[name] = jnp.asarray(drawn.astype(out[name].dtype))
    for name, factor in factors.items():
        out[name] = (out[name] * factor).astype(out[name].dtype)
    return out
```

```python
from contextlib import ExitStack

import numpy as np

import concourse.bass as bass
from concourse import mybir

P = 128
ALU = mybir.AluOpType
ACT = mybir.ActivationFunctionType
F32 = mybir.dt.float32
BF16 = mybir.dt.bfloat16
I32 = mybir.dt.int32
U32 = mybir.dt.uint32
U8 = mybir.dt.uint8

MASKED = -1.0e30
LN_EPS = 1.0e-5
CAP = 256
TOPK = 8


class Chain:

    def __init__(self, eng, sem):
        self.eng, self.sem, self.base, self.n = eng, sem, 0, 0

    def link(self, ins):
        self.mark(ins)
        self.wait()

    def mark(self, ins):
        ins.then_inc(self.sem, 1)
        self.n += 1

    def wait(self):
        self.eng.wait_ge(self.sem, self.base + self.n)

    def enter(self, passes_before, per_pass):
        self.start = self.base + self.n
        self.base, self.n = self.start + passes_before * per_pass, 0

    def leave(self, passes, per_pass):
        assert self.n == per_pass, (self.n, per_pass)
        self.base, self.n = self.start + passes * per_pass, 0


def flamingo_moe(nc, x, ctxT, mask, kpm, g_x, g_f, wqT, bqT, wkT, bkT, gwT, wg, wu, wd, out):
    B, CP, CC, S = ctxT.shape
    T, H = x.shape
    E, _, KH, I = wg.shape
    MI = I // P
    TB = S // P
    NH = 512
    D = CC * P
    HW = H + E
    BIG = 65536.0
    KEY0 = BIG * E
    ROWS = T + CAP
    assert CP == P and KH * P == H == S and CAP == 2 * P and MI * P == I

    h_rows = nc.dram_tensor("h_rows", [ROWS, HW], F32, kind="Internal").ap()
    place_table = nc.dram_tensor("place_table", [CAP * E, 1], I32, kind="Internal").ap()

    with ExitStack() as ctx:
        def sem(name):
            return ctx.enter_context(nc.semaphore(name))

        def sb(name, shape, dt, where=ctx):
            return where.enter_context(nc.sbuf_tensor(name, shape, dt))

        raw_g = [sb(f"raw_g{u}", [P, KH, I], F32) for u in range(2)]
        raw_u = [sb(f"raw_u{u}", [P, KH, I], F32) for u in range(2)]
        raw_d = sb("raw_d", [P, MI, H], F32)
        ident_bf = sb("ident_bf", [P, P], BF16)
        table = sb("table", [P, 2, E], I32)

        a_mem = ExitStack()
        ident = sb("ident", [P, P], F32, a_mem)
        before = sb("before", [P, P], BF16, a_mem)
        ones = sb("ones", [P, P], BF16, a_mem)
        expert_no = sb("expert_no", [P, E], F32, a_mem)
        free_rows = sb("free_rows", [P, 2, E], I32, a_mem)
        token_no = sb("token_no", [P, 2], I32, a_mem)
        zero_row = sb("zero_row", [P, HW], F32, a_mem)
        gates = sb("gates", [P, 2], F32, a_mem)
        tanh_g = sb("tanh_g", [P, 2], F32, a_mem)
        w_qk = sb("w_qk", [P, 2, CC, D], F32, a_mem)
        b_qk = sb("b_qk", [P, 2, CC], F32, a_mem)
        gw_sb = sb("gw_sb", [P, KH, E], F32, a_mem)
        mask_u8 = sb("mask_u8", [P, TB, S], U8, a_mem)
        mask_add = sb("mask_add", [P, TB, S], BF16, a_mem)
        kpm_u8 = sb("kpm_u8", [P, S], U8, a_mem)
        kpm_add = sb("kpm_add", [P, S], BF16, a_mem)
        both_add = sb("both_add", [P, 2, S], BF16, a_mem)
        ctx_sb = sb("ctx_sb", [P, CC, S], F32, a_mem)
        qk = sb("qk", [P, 2, CC, S], F32, a_mem)
        xb = [sb(f"xb{i}", [P, H], F32, a_mem) for i in range(4)]
        junk = sb("junk", [P, S], BF16, a_mem)
        zb = [sb(f"zb{i}", [P, S], F32, a_mem) for i in range(2)]
        hb = [sb(f"hb{i}", [P, H], F32, a_mem) for i in range(2)]
        hT = sb("hT", [P, KH, P], F32, a_mem)
        hrow = [sb(f"hrow{i}", [P, HW], F32, a_mem) for i in range(4)]
        xsum = sb("xsum", [P, 4], F32, a_mem)
        nmean = sb("nmean", [P, 4], F32, a_mem)
        xssq = sb("xssq", [P, 4], F32, a_mem)
        sc = [sb(f"sc{i}", [P, 16], F32, a_mem) for i in range(2)]
        xscale = [sb(f"xscale{i}", [P, 1], F32, a_mem) for i in range(2)]
        half_pow = sb("half_pow", [P, 1], F32, a_mem)
        xvar = sb("xvar", [P, 1], F32, a_mem)
        norm = [sb(f"norm{i}", [P, 2], F32, a_mem) for i in range(2)]
        psum_p = sb("psum_p", [P, 2], F32, a_mem)
        bn = [sb(f"bn{i}", [P, 2, 6], F32, a_mem) for i in range(2)]
        lg = [sb(f"lg{i}", [P, E], F32, a_mem) for i in range(2)]
        top = [sb(f"top{i}", [P, TOPK], F32, a_mem) for i in range(2)]
        ntop = [sb(f"ntop{i}", [P, 1], F32, a_mem) for i in range(2)]
        left = sb("left", [P, E], F32, a_mem)
        sel = [sb(f"sel{i}", [P, E], BF16, a_mem) for i in range(2)]
        taken = [sb(f"taken{i}", [P, E], BF16, a_mem) for i in range(2)]
        e8 = sb("e8", [P, TOPK], F32, a_mem)
        e8sum = [sb(f"e8sum{i}", [P, 1], F32, a_mem) for i in range(2)]
        ew = [sb(f"ew{i}", [P, E], F32, a_mem) for i in range(2)]
        q_ = sb("q_", [P, E], F32, a_mem)
        fits = sb("fits", [P, E], F32, a_mem)
        place = sb("place", [P, E], F32, a_mem)
        key = sb("key", [P, E], F32, a_mem)
        key8 = sb("key8", [P, TOPK], F32, a_mem)
        r8 = sb("r8", [P, 2], F32, a_mem)
        where8 = [sb(f"where8_{i}", [P, TOPK], I32, a_mem) for i in range(2)]
        a_mem.close()

        split_g = [sb(f"split_g{u}", [P, 2, KH, I], BF16) for u in range(2)]
        split_u = [sb(f"split_u{u}", [P, 2, KH, I], BF16) for u in range(2)]
        split_d = sb("split_d", [P, 2, MI, H], BF16)
        xg = [sb(f"xg{u}", [P, 2, HW], F32) for u in range(2)]
        xT = [sb(f"xT{u}", [P, KH, 2, CAP], BF16) for u in range(2)]
        g_idx = [sb(f"g_idx{u}", [P, 2], I32) for u in range(2)]
        s_idx = [sb(f"s_idx{u}", [P, 2], I32) for u in range(2)]
        wcol = [sb(f"wcol{u}", [P, 2], F32) for u in range(2)]
        sil = sb("sil", [P, MI, CAP], F32)
        prod = sb("prod", [P, MI, CAP], F32)
        act = [sb(f"act{u}", [P, 2, MI, CAP], BF16) for u in range(2)]
        ob = [sb(f"ob{u}", [P, 2, H], F32) for u in range(2)]

        consts_made = sem("consts_made")
        small_loaded = sem("small_loaded")
        mask_loaded = sem("mask_loaded")
        mask_ready = sem("mask_ready")
        tanh_ready = sem("tanh_ready")
        rows_cleared = sem("rows_cleared")
        ctx_loaded = sem("ctx_loaded")
        kpm_loaded = sem("kpm_loaded")
        kpm_ready = sem("kpm_ready")
        proj_done = sem("proj_done")
        proj_out = sem("proj_out")
        scores_done = sem("scores_done")
        scores_used = sem("scores_used")
        x_loaded = [sem(f"x_loaded{i}") for i in range(4)]
        x_summed = sem("x_summed")
        nmean_ready = sem("nmean_ready")
        x_squared = sem("x_squared")
        both_ready = sem("both_ready")
        z_ready = sem("z_ready")
        exp_done = sem("exp_done")
        x1_ready = sem("x1_ready")
        xscale_ready = sem("xscale_ready")
        var_ready = sem("var_ready")
        norm_ready = sem("norm_ready")
        h_done = sem("h_done")
        h_high = sem("h_high")
        h_low = sem("h_low")
        hT_done = sem("hT_done")
        hT_out = sem("hT_out")
        logits_done = sem("logits_done")
        chosen = sem("chosen")
        pos_done = sem("pos_done")
        ew_done = sem("ew_done")
        routed = sem("routed")
        x1_stored = [sem(f"x1_stored{i}") for i in range(4)]
        h_stored = [sem(f"h_stored{i}") for i in range(4)]
        places_stored = [sem(f"places_stored{i}") for i in range(2)]
        table_loaded = sem("table_loaded")
        dve_chain = sem("dve_chain")
        act_chain = sem("act_chain")
        pool_chain = sem("pool_chain")
        g_loaded = [sem(f"g_loaded{u}") for u in range(2)]
        u_loaded = [sem(f"u_loaded{u}") for u in range(2)]
        d_loaded = sem("d_loaded")
        g_high, g_low = sem("g_high"), sem("g_low")
        u_high, u_low = sem("u_high"), sem("u_low")
        d_high, d_low = sem("d_high"), sem("d_low")
        gathered = [sem(f"gathered{u}") for u in range(2)]
        wcol_ready = sem("wcol_ready")
        xT_done = sem("xT_done")
        xT_out = sem("xT_out")
        gu_done = sem("gu_done")
        sil_done = sem("sil_done")
        act_ready = sem("act_ready")
        down_done = sem("down_done")
        down_out = sem("down_out")
        scattered = sem("scattered")

        CONSTS = 10
        SMALL = 7

        p_mem = ExitStack()
        ps = lambda name, shape, dt, where: where.enter_context(nc.psum_tensor(name, shape, dt))
        ps_s = [ps(f"ps_s{i}", [P, S], F32, p_mem) for i in range(2)]
        ps_t = ps("ps_t", [P, KH, P], F32, p_mem)
        ps_l = ps("ps_l", [P, NH], F32, p_mem)
        ps_p = ps("ps_p", [P, NH], F32, p_mem)
        p_mem.close()
        ps_gu = [ps(f"ps_gu{m}", [P, 2, CAP], F32, ctx) for m in range(MI)]
        ps_x = [ps(f"ps_x{i}", [P, 2, 2, CAP], BF16, ctx) for i in range(2)]
        ps_d = [ps(f"ps_d{i}", [P, NH], F32, ctx) for i in range(2)]

        block = ctx.enter_context(nc.Block())

        def attention_done(eng):
            eng.wait_ge(routed, B * TB)
            for i in range(4):
                eng.wait_ge(x1_stored[i], 16 * B * TB // 4)
                eng.wait_ge(h_stored[i], 16 * B * TB // 4)
            for i in range(2):
                eng.wait_ge(places_stored[i], 16 * TOPK * B * TB // 2)

        @block.sync
        def _(sp):
            sp.dma_start(gates[:, 0:1], g_x.partition_broadcast(P)).then_inc(small_loaded, 16)
            sp.dma_start(gates[:, 1:2], g_f.partition_broadcast(P)).then_inc(small_loaded, 16)
            sp.dma_start(w_qk[:, 0], wqT).then_inc(small_loaded, 16)
            sp.dma_start(w_qk[:, 1], wkT).then_inc(small_loaded, 16)
            sp.dma_start(b_qk[:, 0], bqT).then_inc(small_loaded, 16)
            sp.dma_start(b_qk[:, 1], bkT).then_inc(small_loaded, 16)

            def load_ctx(b):
                sp.dma_start(ctx_sb[:], ctxT[bass.ds(b, 1)].rearrange("b p c s -> p (b c) s")).then_inc(ctx_loaded, 16)

            def load_kpm(b):
                sp.dma_start(kpm_u8[:], kpm[bass.ds(b, 1), :].rearrange("b s -> (b s)").partition_broadcast(P)
                             ).then_inc(kpm_loaded, 16)

            def load_x(g, j):
                sp.dma_start(xb[j % 4][:], x[bass.ds(g * P, P), :]).then_inc(x_loaded[j % 4], 16)

            load_ctx(0)
            load_kpm(0)
            load_x(0, 0)
            load_x(1, 1)
            sp.dma_start(mask_u8[:], mask.rearrange("(j p) s -> p j s", p=P)).then_inc(mask_loaded, 16)
            sp.dma_start(gw_sb[:], gwT).then_inc(small_loaded, 16)
            load_x(2, 2)
            sp.wait_ge(consts_made, CONSTS)
            for half in range(2):
                r = slice(T + half * P, T + (half + 1) * P)
                sp.dma_start(h_rows[r, :], zero_row[:]).then_inc(rows_cleared, 16)
                sp.dma_start(out[r, :], zero_row[:, 0:H]).then_inc(rows_cleared, 16)
            sp.dma_start(place_table.rearrange("(p k) o -> p (k o)", p=P),
                         free_rows[:].rearrange("p t e -> p (t e)")).then_inc(rows_cleared, 16)

            def load_expert(e, u):
                sp.dma_start(raw_g[u][:], wg[bass.ds(e, 1)].rearrange("e p k i -> p (e k) i")).then_inc(g_loaded[u], 16)
                sp.dma_start(raw_u[u][:], wu[bass.ds(e, 1)].rearrange("e p k i -> p (e k) i")).then_inc(u_loaded[u], 16)

            def load_down(e):
                sp.dma_start(raw_d[:], wd[bass.ds(e, 1)].rearrange("e p m h -> p (e m) h")).then_inc(d_loaded, 16)

            def store_h(g, j):
                sp.wait_ge(routed, g + 1)
                sp.wait_ge(h_low, g + 1)
                sp.dma_start(h_rows[bass.ds(g * P, P), :], hrow[j % 4][:]).then_inc(h_stored[j % 4], 16)

            def batch(b, first, last):
                for j in range(TB):
                    g = b * TB + j
                    sp.wait_ge(x1_ready, g + 1)
                    sp.dma_start(out[bass.ds(g * P, P), :], xb[j % 4][:]).then_inc(x1_stored[j % 4], 16)
                    if not (first and j < 2):
                        store_h(g - 2, (j + 6) % TB)
                    if not (last and j >= TB - 3):
                        if not (first and j < 1):
                            use = b * 2 + (j + 3) // 4
                            sp.wait_ge(x1_stored[(j + 3) % 4], 16 * use)
                            sp.wait_ge(h_high, g)
                        load_x(g + 3, j + 3)
                    if j == 0 and not last:
                        sp.wait_ge(proj_done, (b + 1) * 8)
                        load_ctx(b + 1)
                    if j == 1 and not last:
                        sp.wait_ge(kpm_ready, b + 1)
                        load_kpm(b + 1)

            batch(0, True, False)
            load_expert(0, 0)
            load_down(0)
            for b in range(1, B - 1):
                batch(b, False, False)
            load_expert(1, 1)
            batch(B - 1, False, True)
            for g in (B * TB - 2, B * TB - 1):
                store_h(g, g % TB)
            for i in range(2):
                sp.wait_ge(places_stored[i], 16 * TOPK * B * TB // 2)
            sp.dma_start(table[:].rearrange("p t e -> p (t e)"),
                         place_table.rearrange("(p k) o -> p (k o)", p=P)).then_inc(table_loaded, 16)

            def expert(e, u, ahead):
                if ahead >= 1:
                    sp.wait_ge(d_low, e + 1)
                    load_down(e + 1)
                if ahead >= 2:
                    sp.wait_ge(g_low, e + 1)
                    sp.wait_ge(u_low, e + 1)
                    load_expert(e + 2, u)

            with sp.Fori(0, E // 2 - 1) as i:
                expert(2 * i, 0, 2)
                expert(2 * i + 1, 1, 2)
            expert(E - 2, 0, 1)
            sp.wait_ge(scattered, 32 * E)

        @block.tensor
        def _(pe):
            def project(b):
                pe.wait_ge(ctx_loaded, 16 * (b + 1))
                for c in range(8):
                    which, o, n = c // 4, c // 2 % 2, c % 2
                    if c >= 2:
                        pe.wait_ge(proj_out, b * 8 + c - 1)
                    for k in range(CC):
                        mm = pe.matmul(ps_s[0][:, n * NH:(n + 1) * NH], w_qk[:, which, k, o * P:(o + 1) * P],
                                       ctx_sb[:, k, n * NH:(n + 1) * NH], start=(k == 0), stop=(k == CC - 1))
                    mm.then_inc(proj_done, 1)
                pe.wait_ge(proj_out, b * 8 + 8)

            def scores(j):
                for n in range(S // NH):
                    for k in range(CC):
                        mm = pe.matmul(ps_s[j % 2][:, n * NH:(n + 1) * NH], qk[:, 0, k, j * P:(j + 1) * P],
                                       qk[:, 1, k, n * NH:(n + 1) * NH], start=(k == 0), stop=(k == CC - 1))
                mm.then_inc(scores_done, 1)

            def logits(g, j):
                pe.wait_ge(h_done, g + 1)
                if not isinstance(g, int) or g > 0:
                    pe.wait_ge(hT_out, g)
                for k in range(KH):
                    mm = pe.transpose(ps_t[:, k, :], hb[j % 2][:, k * P:(k + 1) * P], ident[:])
                mm.then_inc(hT_done, 1)
                pe.wait_ge(hT_out, g + 1)
                if not isinstance(g, int) or g > 0:
                    pe.wait_ge(chosen, g)
                for k in range(KH):
                    mm = pe.matmul(ps_l[:, 0:E], hT[:, k, :], gw_sb[:, k, :], start=(k == 0), stop=(k == KH - 1))
                mm.then_inc(logits_done, 1)

            def positions(g, j):
                pe.wait_ge(chosen, g + 1)
                if not isinstance(g, int) or g > 0:
                    pe.wait_ge(routed, g)
                pe.matmul(ps_p[:, 0:E], before[:], sel[j % 2][:], start=True, stop=False)
                pe.matmul(ps_p[:, 0:E], ones[:], taken[j % 2][:], start=False, stop=True).then_inc(pos_done, 1)

            def batch(b, first, last):
                for j in range(TB):
                    g = b * TB + j
                    if j < TB - 1:
                        if not (first and j == 0):
                            pe.wait_ge(scores_used, g)
                        scores(j + 1)
                    if not (first and j == 0):
                        logits(g - 1, j - 1 if j else TB - 1)
                    if j == TB - 1 and not last:
                        pe.wait_ge(scores_used, g)
                        project(b + 1)
                        scores(0)
                    if not (first and j == 0):
                        positions(g - 1, j - 1 if j else TB - 1)

            pe.wait_ge(small_loaded, 16 * SMALL)
            pe.wait_ge(consts_made, CONSTS)
            project(0)
            scores(0)
            batch(0, True, False)
            for b in range(1, B - 1):
                batch(b, False, False)
            batch(B - 1, False, True)
            logits(B * TB - 1, TB - 1)
            positions(B * TB - 1, TB - 1)

            def turn(e, u, first=False):
                pe.wait_ge(gathered[u], 16 * (e - u) + 32)
                xv = [xg[u][:, half, 0:H].bitcast(BF16) for half in range(2)]
                for q in range(4):
                    if not (first and q < 2):
                        pe.wait_ge(xT_out, 4 * e + q - 1)
                    for kk in range(2):
                        for hl in range(2):
                            for half in range(2):
                                at = hl * H + (2 * q + kk) * P
                                mm = pe.transpose(ps_x[q % 2][:, kk, hl, half * P:(half + 1) * P],
                                                  xv[half][:, at:at + P], ident_bf[:])
                    mm.then_inc(xT_done, 1)

            PAIRS = ((0, 0), (0, 1), (1, 0))

            def gate_up(e, u, first):
                pe.wait_ge(xT_out, 4 * e + 4)
                for m in range(MI):
                    if not first:
                        pe.wait_ge(act_ready, MI * e - MI + m + 1)
                    for t, w in ((0, split_g[u]), (1, split_u[u])):
                        if m == 0:
                            pe.wait_ge((g_low, u_low)[t], e + 1)
                        for k in range(KH):
                            for wi, xi in PAIRS:
                                mm = pe.matmul(ps_gu[m][:, t, :], w[:, wi, k, m * P:(m + 1) * P], xT[u][:, k, xi, :],
                                               start=(k == 0 and (wi, xi) == (0, 0)),
                                               stop=(k == KH - 1 and (wi, xi) == (1, 0)))
                    mm.then_inc(gu_done, 1)

            def down(e, u, first):
                pe.wait_ge(d_low, e + 1)
                pe.wait_ge(act_ready, MI * e + MI)
                for n in range(4):
                    half, c = n // 2, n % 2
                    if not (first and n < 2):
                        pe.wait_ge(down_out, 4 * e + n - 1)
                    for m in range(MI):
                        for wi, ai in PAIRS:
                            mm = pe.matmul(ps_d[n % 2][:], act[u][:, ai, m, half * P:(half + 1) * P],
                                           split_d[:, wi, m, c * NH:(c + 1) * NH],
                                           start=(m == 0 and (wi, ai) == (0, 0)),
                                           stop=(m == MI - 1 and (wi, ai) == (1, 0)))
                    mm.then_inc(down_done, 1)

            attention_done(pe)
            turn(0, 0, True)
            gate_up(0, 0, True)
            turn(1, 1)
            down(0, 0, True)

            def expert(e, u, last=False):
                gate_up(e, u, False)
                if not last:
                    turn(e + 1, 1 - u)
                down(e, u, False)

            with pe.Fori(0, E // 2 - 1) as i:
                expert(2 * i + 1, 1)
                expert(2 * i + 2, 0)
            expert(E - 1, 1, True)

        @block.scalar
        def _(s):
            chain = Chain(s, act_chain)
            s.wait_ge(small_loaded, 16 * SMALL)
            s.activation(tanh_g[:], gates[:], ACT.Tanh).then_inc(tanh_ready, 1)

            def project_out(b):
                for c in range(8):
                    which, o, n = c // 4, c // 2 % 2, c % 2
                    s.wait_ge(proj_done, b * 8 + c + 1)
                    s.activation(qk[:, which, o, n * NH:(n + 1) * NH], ps_s[0][:, n * NH:(n + 1) * NH], ACT.Identity,
                                 bias=b_qk[:, which, o:o + 1]).then_inc(proj_out, 1)

            def x_square(g, j):
                s.wait_ge(nmean_ready, g + 1)
                s.wait_ge(x_summed, max(g + 1, 2))
                s.activation(junk[:], xb[j % 4][:], ACT.Square, bias=nmean[:, j % 4:j % 4 + 1],
                             accum_out=xssq[:, j % 4:j % 4 + 1]).then_inc(x_squared, 1)

            def batch(b, first, last):
                for j in range(TB):
                    g = b * TB + j
                    if not (first and j < 2):
                        jj = (j + 6) % TB
                        s.wait_ge(chosen, g - 1)
                        expert_weights(g - 2, jj, first and j == 2)
                    if not (first and j < 1):
                        h_out(g - 1)
                    s.wait_ge(z_ready, g + 1)
                    s.activation(zb[j % 2][:], zb[j % 2][:], ACT.Exp, bias=sc[j % 2][:, 2:3], scale=xscale[j % 2][:],
                                 accum_out=psum_p[:, j % 2:j % 2 + 1]).then_inc(exp_done, 1)
                    if not (last and j == TB - 1):
                        x_square(g + 1, j + 1)
                    if not (last and j >= TB - 2):
                        s.wait_ge(x_loaded[(j + 2) % 4], 16 * (2 * b + (j + 2) // 4 + 1))
                        s.wait_ge(x_squared, g + 2)
                        s.activation(junk[:], xb[(j + 2) % 4][:], ACT.Identity,
                                     accum_out=xsum[:, (j + 2) % 4:(j + 2) % 4 + 1]).then_inc(x_summed, 1)
                    if j == TB - 1 and not last:
                        project_out(b + 1)
                    s.wait_ge(norm_ready, g + 1)
                    if not (first and j < 2):
                        s.wait_ge(hT_done, g - 1)
                        s.wait_ge(h_low, g - 1)
                    s.activation(hb[j % 2][:], xb[j % 4][:], ACT.Identity, bias=norm[j % 2][:, 1:2],
                                 scale=norm[j % 2][:, 0:1]).then_inc(h_done, 1)
                    if not (first and j < 4):
                        s.wait_ge(h_stored[j % 4], 16 * (2 * b + j // 4))
                    s.activation(hrow[j % 4][:].bitcast(BF16)[:, 0:H], xb[j % 4][:], ACT.Identity,
                                 bias=norm[j % 2][:, 1:2], scale=norm[j % 2][:, 0:1]).then_inc(h_high, 1)

            def expert_weights(g, jj, first=False):
                if not first:
                    s.wait_ge(ew_done, g)
                s.activation(e8[:], top[jj % 2][:], ACT.Exp, bias=ntop[jj % 2][:], accum_out=e8sum[jj % 2][:])
                s.activation(ew[jj % 2][:], lg[jj % 2][:], ACT.Exp, bias=ntop[jj % 2][:]).then_inc(ew_done, 1)

            def h_out(g):
                s.wait_ge(hT_done, g + 1)
                if not isinstance(g, int) or g > 0:
                    s.wait_ge(logits_done, g)
                s.activation(hT[:], ps_t[:], ACT.Copy).then_inc(hT_out, 1)

            project_out(0)
            for j in range(2):
                s.wait_ge(x_loaded[j], 16)
                if j:
                    s.wait_ge(x_summed, j)
                s.activation(junk[:], xb[j][:], ACT.Identity, accum_out=xsum[:, j:j + 1]).then_inc(x_summed, 1)
            x_square(0, 0)
            batch(0, True, False)
            for b in range(1, B - 1):
                batch(b, False, False)
            batch(B - 1, False, True)
            N = B * TB
            h_out(N - 1)
            for g in (N - 2, N - 1):
                s.wait_ge(chosen, g + 1)
                expert_weights(g, g % TB)

            attention_done(s)

            def high(dst, src, loaded, value, done):
                s.wait_ge(loaded, value)
                s.activation(dst, src, ACT.Copy).then_inc(done, 1)

            def gate_high(e, u, first=False):
                if not first:
                    s.wait_ge(gu_done, MI * e - MI)
                high(split_g[u][:, 0], raw_g[u][:], g_loaded[u], 8 * (e - u) + 16, g_high)

            def up_high(e, u, first=False):
                high(split_u[u][:, 0], raw_u[u][:], u_loaded[u], 8 * (e - u) + 16, u_high)

            def down_high(e, first=False):
                if not first:
                    s.wait_ge(down_done, 4 * e)
                high(split_d[:, 0], raw_d[:], d_loaded, 16 * e + 16, d_high)

            def silu(e, m, first=False):
                s.wait_ge(gu_done, MI * e + m + 1)
                s.activation(sil[:, m], ps_gu[m][:, 0], ACT.Silu).then_inc(sil_done, 1)

            def rows_out(e, u, first=False):
                s.wait_ge(wcol_ready, e + 1)
                if not first:
                    s.wait_ge(scattered, 32 * e - 32)
                for n in range(4):
                    s.wait_ge(down_done, 4 * e + n + 1)
                    s.activation(ob[u][:, n // 2, n % 2 * NH:(n % 2 + 1) * NH], ps_d[n % 2][:], ACT.Copy,
                                 scale=wcol[u][:, n // 2:n // 2 + 1]).then_inc(down_out, 1)

            def expert(e, u, first=0, last=False):
                down_high(e, first == 1)
                silu(e, 0)
                if not last:
                    gate_high(e + 1, 1 - u, first == 1)
                silu(e, 1)
                if not last:
                    up_high(e + 1, 1 - u)
                silu(e, 2)
                rows_out(e, u, first > 0)

            gate_high(0, 0, True)
            up_high(0, 0, True)
            expert(0, 0, 1)
            expert(1, 1, 2)
            with s.Fori(1, E // 2 - 1) as i:
                expert(2 * i, 0)
                expert(2 * i + 1, 1)
            expert(E - 2, 0)
            expert(E - 1, 1, 0, True)

        @block.vector
        def _(v):
            chain = Chain(v, dve_chain)

            def chose(g, j):
                u = j % 2
                v.wait_ge(logits_done, g + 1)
                if not isinstance(g, int) or g >= 2:
                    v.wait_ge(ew_done, g - 1)
                    v.wait_ge(pos_done, g - 1)
                chain.link(v.tensor_copy(lg[u][:], ps_l[:, 0:E]))
                chain.link(v.max(top[u][:], lg[u][:]))
                v.tensor_scalar(ntop[u][:], top[u][:, 0:1], -1.0, None, ALU.mult)
                chain.link(v.match_replace(left[:], top[u][:], lg[u][:], -3.0e38))
                chain.link(v.tensor_scalar(sel[u][:], left[:], -3.0e38, None, ALU.is_le))
                if not isinstance(g, int) or g >= 1:
                    v.wait_ge(pos_done, g)
                v.tensor_tensor(taken[1 - u][:], taken[u][:], sel[u][:], ALU.add).then_inc(chosen, 1)

            def route(g, j):
                u = j % 2
                v.wait_ge(pos_done, g + 1)
                chain.link(v.scalar_tensor_tensor(q_[:], sel[u][:], -BIG, ps_p[:, 0:E], ALU.mult, ALU.add))
                v.tensor_scalar(fits[:], q_[:], CAP - BIG, None, ALU.is_lt)
                chain.link(v.scalar_tensor_tensor(place[:], q_[:], float(E), expert_no[:], ALU.mult, ALU.add))
                chain.link(v.scalar_tensor_tensor(key[:], place[:], -1.0, fits[:], ALU.mult, ALU.mult))
                chain.link(v.max(key8[:], key[:]))
                if not isinstance(g, int) or g >= 2:
                    v.wait_ge(places_stored[u], 8 * TOPK * (g - u))
                v.tensor_scalar(where8[u][:], key8[:], -1.0, KEY0, ALU.mult, ALU.add)
                v.wait_ge(ew_done, g + 1)
                chain.link(v.reciprocal(r8[:, 0:1], e8sum[u][:]))
                chain.link(v.tensor_tensor(r8[:, 1:2], r8[:, 0:1], tanh_g[:, 1:2], ALU.mult))
                if not isinstance(g, int) or g >= 4:
                    v.wait_ge(h_stored[j % 4], 4 * (g - j % 4))
                v.scalar_tensor_tensor(hrow[j % 4][:, H:HW], ew[u][:], r8[:, 1:2], fits[:], ALU.mult,
                                       ALU.mult).then_inc(routed, 1)

            def minus_mean(g, j):
                v.wait_ge(x_summed, g + 1)
                v.tensor_scalar(nmean[:, j % 4:j % 4 + 1], xsum[:, j % 4:j % 4 + 1], -1.0 / H, None,
                                ALU.mult).then_inc(nmean_ready, 1)

            def batch(b, first, last):
                for j in range(TB):
                    g = b * TB + j
                    u, f = j % 2, j % 4
                    c = sc[u]
                    if not (first and j < 2):
                        v.wait_ge(h_high, g - 1)
                    v.wait_ge(nmean_ready, g + 1)
                    v.wait_ge(x_squared, g + 1)
                    v.wait_ge(scores_done, g + 1)
                    ins = v.scalar_tensor_tensor(zb[u][:], xb[f][:], nmean[:, f:f + 1], ps_s[u][:], ALU.add, ALU.mult)
                    ins.then_inc(scores_used, 1)
                    v.wait_ge(scores_used, g + 1)
                    v.wait_ge(both_ready, g + 1)
                    chain.link(v.tensor_tensor_reduce(zb[u][:], zb[u][:], both_add[:, u], 1.0, -3.0e38, ALU.add, ALU.max,
                                                      c[:, 3:4]))
                    v.wait_ge(xscale_ready, g + 1)
                    v.scalar_tensor_tensor(c[:, 2:3], c[:, 3:4], -1.0, xscale[u][:], ALU.mult, ALU.mult).then_inc(z_ready, 1)
                    if not (first and j < 2):
                        route(g - 2, (j + 6) % TB)
                    v.wait_ge(exp_done, g + 1)
                    chain.link(v.reciprocal(c[:, 4:5], psum_p[:, u:u + 1]))
                    chain.link(v.tensor_tensor(c[:, 5:6], c[:, 4:5], tanh_g[:, 0:1], ALU.mult))
                    v.scalar_tensor_tensor(xb[f][:], zb[u][:], c[:, 5:6], xb[f][:], ALU.mult, ALU.add).then_inc(x1_ready, 1)
                    v.wait_ge(x1_ready, g + 1)
                    for n in range(2):
                        st = v.bn_stats(bn[u][:, n], xb[f][:, n * NH:(n + 1) * NH])
                    chain.link(st)
                    chain.link(v.bn_aggr(c[:, 10:12], bn[u][:].rearrange("p a b -> p (a b)")))
                    v.tensor_scalar(c[:, 9:10], c[:, 10:11], -1.0, None, ALU.mult)
                    v.tensor_scalar(c[:, 6:7], c[:, 11:12], LN_EPS, None, ALU.add).then_inc(var_ready, 1)
                    if not (last and j >= TB - 2):
                        minus_mean(g + 2, j + 2)
                    if not (first and j < 1):
                        chose(g - 1, (j + 7) % TB)

            chain.link(v.memset(taken[0][:], 0.0))
            v.wait_ge(tanh_ready, 1)
            v.wait_ge(consts_made, CONSTS)
            minus_mean(0, 0)
            minus_mean(1, 1)
            batch(0, True, False)
            for b in range(1, B - 1):
                batch(b, False, False)
            batch(B - 1, False, True)
            N = B * TB
            route(N - 2, TB - 2)
            chose(N - 1, TB - 1)
            route(N - 1, TB - 1)

            attention_done(v)

            def low(dst, src, high, high_done, e, done):
                v.wait_ge(high_done, e + 1)
                v.tensor_tensor(dst, src, high, ALU.subtract).then_inc(done, 1)

            def gate_low(e, u):
                low(split_g[u][:, 1], raw_g[u][:], split_g[u][:, 0], g_high, e, g_low)

            def up_low(e, u):
                low(split_u[u][:, 1], raw_u[u][:], split_u[u][:, 0], u_high, e, u_low)

            def down_low(e):
                low(split_d[:, 1], raw_d[:], split_d[:, 0], d_high, e, d_low)

            def activate(e, u, m, first):
                v.wait_ge(sil_done, MI * e + m + 1)
                if m == 0 and not first:
                    v.wait_ge(down_done, 4 * e - 4)
                chain.link(v.tensor_tensor(prod[:, m], sil[:, m], ps_gu[m][:, 1], ALU.mult))
                chain.link(v.tensor_copy(act[u][:, 0, m], prod[:, m]))
                v.tensor_tensor(act[u][:, 1, m], prod[:, m], act[u][:, 0, m], ALU.subtract).then_inc(act_ready, 1)

            def turn_out(e, u, first=False):
                for q in range(4):
                    v.wait_ge(xT_done, 4 * e + q + 1)
                    v.tensor_copy(xT[u][:, 2 * q:2 * q + 2], ps_x[q % 2][:]).then_inc(xT_out, 1)

            def expert(e, u, first=False, last=False):
                down_low(e)
                activate(e, u, 0, first)
                if not last:
                    gate_low(e + 1, 1 - u)
                activate(e, u, 1, first)
                if not last:
                    up_low(e + 1, 1 - u)
                activate(e, u, 2, first)
                if not last:
                    turn_out(e + 1, 1 - u)

            gate_low(0, 0)
            up_low(0, 0)
            turn_out(0, 0)
            expert(0, 0, True)
            expert(1, 1, True)
            with v.Fori(1, E // 2 - 1) as i:
                chain.enter(i - 1, 12)
                expert(2 * i, 0)
                expert(2 * i + 1, 1)
                chain.leave(E // 2 - 2, 12)
            expert(E - 2, 0)
            expert(E - 1, 1, False, True)

        @block.gpsimd
        def _(p):
            chain = Chain(p, pool_chain)
            p.memset(ones[:], 1.0).then_inc(consts_made, 1)
            p.memset(zero_row[:], 0.0).then_inc(consts_made, 1)
            p.memset(half_pow[:], -0.5).then_inc(consts_made, 1)
            chain.mark(p.memset(ident[:], 0.0))
            chain.mark(p.memset(ident_bf[:], 0.0))
            chain.mark(p.memset(before[:], 1.0))
            p.iota(free_rows[:], pattern=[[1, 2], [0, E]], base=T, channel_multiplier=2).then_inc(consts_made, 1)
            p.iota(token_no[:, 0:1], pattern=[[0, 1]], base=0, channel_multiplier=1).then_inc(consts_made, 1)
            p.iota(token_no[:, 1:2], pattern=[[0, 1]], base=P, channel_multiplier=1).then_inc(consts_made, 1)
            p.iota(expert_no[:], pattern=[[1, E]], base=0, channel_multiplier=0,
                   allow_small_or_imprecise_dtypes=True).then_inc(consts_made, 1)
            chain.wait()
            for t in (ident, ident_bf):
                p.affine_select(out=t[:], in_=t[:], compare_op=ALU.not_equal, fill=1.0, base=0,
                                pattern=[[-1, P]], channel_multiplier=1).then_inc(consts_made, 1)
            p.affine_select(out=before[:], in_=before[:], compare_op=ALU.is_gt, fill=0.0, base=0,
                            pattern=[[1, P]], channel_multiplier=-1).then_inc(consts_made, 1)
            p.wait_ge(mask_loaded, 16)
            for j in range(TB):
                p.tensor_scalar(mask_add[:, j], mask_u8[:, j], MASKED, None, ALU.mult).then_inc(mask_ready, 1)

            def key_mask(b):
                p.wait_ge(kpm_loaded, 16 * (b + 1))
                p.tensor_scalar(kpm_add[:], kpm_u8[:], MASKED, None, ALU.mult).then_inc(kpm_ready, 1)
                p.wait_ge(kpm_ready, b + 1)

            def both(g, j, first=False):
                if not first:
                    p.wait_ge(z_ready, g - 1)
                p.wait_ge(mask_ready, j % TB + 1)
                p.tensor_tensor(both_add[:, j % 2], mask_add[:, j % TB], kpm_add[:], ALU.add).then_inc(both_ready, 1)

            def x_scale(g, j):
                p.wait_ge(x_squared, g + 1)
                if not isinstance(g, int) or g >= 2:
                    p.wait_ge(exp_done, g - 1)
                chain.link(p.tensor_scalar(xvar[:], xssq[:, j % 4:j % 4 + 1], D / H, D * LN_EPS, ALU.mult, ALU.add))
                p.tensor_tensor(xscale[j % 2][:], xvar[:], half_pow[:], ALU.pow).then_inc(xscale_ready, 1)

            def x1_norm(g, j):
                u = j % 2
                p.wait_ge(var_ready, g + 1)
                if not isinstance(g, int) or g >= 2:
                    p.wait_ge(h_high, g - 1)
                chain.link(p.tensor_tensor(norm[u][:, 0:1], sc[u][:, 6:7], half_pow[:], ALU.pow))
                p.tensor_tensor(norm[u][:, 1:2], sc[u][:, 9:10], norm[u][:, 0:1], ALU.mult).then_inc(norm_ready, 1)

            def scatter_places(g, j):
                u = j % 2
                p.wait_ge(routed, g + 1)
                for k in range(TOPK):
                    p.indirect_dma_start(
                        out=place_table, out_offset=bass.IndirectOffsetOnAxis(ap=where8[u][:, k:k + 1].bitcast(U32), axis=0),
                        in_=token_no[:, u:u + 1], in_offset=None, bounds_check=CAP * E - 1, oob_is_err=False,
                    ).then_inc(places_stored[u], 16)

            def next_tokens(g, j):
                u = j % 2
                p.wait_ge(places_stored[u], 8 * TOPK * (g - u) + 16 * TOPK)
                chain.link(p.tensor_scalar(token_no[:, u:u + 1], token_no[:, u:u + 1], 2 * P, None, ALU.add))

            def batch(b, first, last):
                for j in range(TB):
                    g = b * TB + j
                    if j < TB - 1:
                        both(g + 1, j + 1, first and j < 1)
                    elif not last:
                        p.wait_ge(both_ready, g + 1)
                        key_mask(b + 1)
                        both(g + 1, 0)
                    if not (last and j == TB - 1):
                        x_scale(g + 1, j + 1)
                    x1_norm(g, j)
                    if not (first and j < 3):
                        next_tokens(g - 3, (j + 5) % TB)
                    if not (first and j < 2):
                        scatter_places(g - 2, (j + 6) % TB)
                    p.wait_ge(h_high, g + 1)
                    p.wait_ge(h_done, g + 1)
                    row = hrow[j % 4][:].bitcast(BF16)
                    p.tensor_tensor(row[:, H:2 * H], hb[j % 2][:], row[:, 0:H], ALU.subtract).then_inc(h_low, 1)

            key_mask(0)
            both(0, 0, True)
            p.wait_ge(consts_made, CONSTS)
            x_scale(0, 0)
            p.wait_ge(rows_cleared, 16 * 5)
            batch(0, True, False)
            for b in range(1, B - 1):
                batch(b, False, False)
            batch(B - 1, False, True)
            N = B * TB
            scatter_places(N - 2, TB - 2)
            next_tokens(N - 3, TB - 3)
            scatter_places(N - 1, TB - 1)

            attention_done(p)
            p.wait_ge(table_loaded, 16)

            last_row = p.alloc_register("last_row")
            p.reg_mov(last_row, ROWS - 1)

            def hold():
                p.reg_alu(last_row, last_row, ROWS - 1, op=ALU.min)

            def gather(e, u):
                chain.link(p.tensor_copy(g_idx[u][:], table[:, :, bass.ds(e, 1)].rearrange("p t e -> p (t e)")))
                hold()
                for half in range(2):
                    p.indirect_dma_start(
                        out=xg[u][:, half, :], out_offset=None, in_=h_rows,
                        in_offset=bass.IndirectOffsetOnAxis(ap=g_idx[u][:, half:half + 1].bitcast(U32), axis=0),
                        bounds_check=last_row, oob_is_err=True,
                    ).then_inc(gathered[u], 16)

            def weights(e, u, first=False):
                p.wait_ge(gathered[u], 16 * (e - u) + 32)
                if not first:
                    p.wait_ge(down_out, 4 * e - 4)
                    p.wait_ge(scattered, 32 * e - 32)
                p.tensor_copy(wcol[u][:], xg[u][:, :, bass.ds(e + H, 1)].rearrange("p t e -> p (t e)")
                              ).then_inc(wcol_ready, 1)
                chain.link(p.tensor_copy(s_idx[u][:], g_idx[u][:]))

            def add_rows(e, u, first=False):
                p.wait_ge(down_out, 4 * e + 4)
                if not first:
                    p.wait_ge(scattered, 32 * e)
                hold()
                for half in range(2):
                    p.indirect_dma_start(
                        out=out, out_offset=bass.IndirectOffsetOnAxis(ap=s_idx[u][:, half:half + 1].bitcast(U32), axis=0),
                        in_=ob[u][:, half, :], in_offset=None, bounds_check=last_row, oob_is_err=True,
                        compute_op=ALU.add,
                    ).then_inc(scattered, 16)

            def expert(e, u, first=0, ahead=2):
                if ahead >= 2:
                    p.wait_ge(xT_done, 4 * e + 4)
                    p.wait_ge(wcol_ready, e + 1)
                    gather(e + 2, u)
                if ahead >= 1:
                    weights(e + 1, 1 - u, first == 1)
                add_rows(e, u, first == 1)

            gather(0, 0)
            gather(1, 1)
            weights(0, 0, True)
            expert(0, 0, 1)
            expert(1, 1)
            with p.Fori(1, E // 2 - 1) as i:
                chain.enter(i - 1, 4)
                expert(2 * i, 0)
                expert(2 * i + 1, 1)
                chain.leave(E // 2 - 2, 4)
            expert(E - 2, 0, 0, 1)
            expert(E - 1, 1, 0, 0)


def kernel(**inputs):
    import concourse.bacc as bacc
    from concourse.bass_utils import run_bass_kernel_spmd

    a = {k: np.asarray(v) for k, v in inputs.items()}
    B, S, H = a["x"].shape
    E, _, I = a["L0_ffn_wg"].shape
    D = a["ctx_512"].shape[2]

    def tiles(w, axis):
        shape = w.shape[:axis] + (w.shape[axis] // P, P) + w.shape[axis + 1:]
        return w.reshape(shape).swapaxes(axis, axis + 1)

    arrays = {
        "x": a["x"].reshape(B * S, H),
        "ctxT": tiles(a["ctx_512"].transpose(0, 2, 1), 1),
        "mask": a["mask_SxS2_bk1"],
        "kpm": a["mask_BxS2_bf0"],
        "g_x": a["g_xattn"], "g_f": a["g_ffn"],
        "wqT": tiles(a["L0_xattn_Wq"].T, 0), "bqT": tiles(a["L0_xattn_bq"], 0),
        "wkT": tiles(a["L0_xattn_Wk"].T, 0), "bkT": tiles(a["L0_xattn_bk"], 0),
        "gwT": tiles(a["L0_ffn_gate_w"].T, 0),
        "wg": tiles(a["L0_ffn_wg"], 1), "wu": tiles(a["L0_ffn_wu"], 1), "wd": tiles(a["L0_ffn_wd"], 1),
    }
    nc = bacc.Bacc("TRN2", target_bir_lowering=False, num_devices=1)
    sent, aps = {}, []
    for name, v in arrays.items():
        v = np.ascontiguousarray(v)
        sent[f"in_{name}"] = v
        aps.append(nc.dram_tensor(f"in_{name}", v.shape, mybir.dt.from_np(v.dtype), kind="ExternalInput").ap())
    out = nc.dram_tensor("out", (B * S + CAP, H), F32, kind="ExternalOutput").ap()
    flamingo_moe(nc, *aps, out)
    r = run_bass_kernel_spmd(nc, [sent], core_ids=[0])
    return r.results[0]["out"][:B * S].reshape(B, S, H)
```

```python
from contextlib import ExitStack

import numpy as np

import concourse.bass as bass
from concourse import mybir

P = 128
ALU = mybir.AluOpType
ACT = mybir.ActivationFunctionType
F32 = mybir.dt.float32
BF16 = mybir.dt.bfloat16
I32 = mybir.dt.int32
U32 = mybir.dt.uint32
U8 = mybir.dt.uint8

MASKED = -1.0e30
LN_EPS = 1.0e-5
CAP = 256
TOPK = 8


class Chain:

    def __init__(self, eng, sem):
        self.eng, self.sem, self.base, self.n = eng, sem, 0, 0

    def mark(self, ins):
        ins.then_inc(self.sem, 1)
        self.n += 1
        return self.base + self.n

    def wait(self, value):
        self.eng.wait_ge(self.sem, value)

    def link(self, ins):
        self.wait(self.mark(ins))

    def enter(self, passes_before, per_pass):
        self.start = self.base + self.n
        self.base, self.n = self.start + passes_before * per_pass, 0

    def leave(self, passes, per_pass):
        assert self.n == per_pass, (self.n, per_pass)
        self.base, self.n = self.start + passes * per_pass, 0


def flamingo_moe(nc, x, ctxT, mask, kpm, g_x, g_f, wqT, bqT, wkT, bkT, gwT, wg, wu, wd, out):
    B, CP, CC, S = ctxT.shape
    T, H = x.shape
    E, _, KH, I = wg.shape
    MI = I // P
    TB = S // P
    NH = 512
    D = CC * P
    HW = H + E
    N = B * TB
    BIG = 65536.0
    KEY0 = BIG * E
    ROWS = T + CAP
    assert CP == P and KH * P == H == S and CAP == 2 * P and MI * P == I

    h_rows = nc.dram_tensor("h_rows", [ROWS, HW], F32, kind="Internal").ap()
    place_table = nc.dram_tensor("place_table", [CAP * E, 1], I32, kind="Internal").ap()

    with ExitStack() as ctx:
        def sem(name):
            return ctx.enter_context(nc.semaphore(name))

        def sb(name, shape, dt, where=ctx):
            return where.enter_context(nc.sbuf_tensor(name, shape, dt))

        raw_g = [sb(f"raw_g{u}", [P, KH, I], F32) for u in range(2)]
        raw_u = [sb(f"raw_u{u}", [P, KH, I], F32) for u in range(2)]
        raw_d = sb("raw_d", [P, MI, H], F32)
        ident = sb("ident", [P, P], F32)
        table = sb("table", [P, 2, E], I32)
        token_no = sb("token_no", [P, 2], I32)
        where8 = [sb(f"where8_{i}", [P, TOPK], I32) for i in range(2)]

        a_mem = ExitStack()
        before = sb("before", [P, P], BF16, a_mem)
        ones = sb("ones", [P, P], BF16, a_mem)
        expert_no = sb("expert_no", [P, E], F32, a_mem)
        free_rows = sb("free_rows", [P, 2, E], I32, a_mem)
        gates = sb("gates", [P, 2], F32, a_mem)
        tanh_g = sb("tanh_g", [P, 2], F32, a_mem)
        w_qk = sb("w_qk", [P, 2, CC, D], F32, a_mem)
        b_qk = sb("b_qk", [P, 2, CC], F32, a_mem)
        gw_sb = sb("gw_sb", [P, KH, E], F32, a_mem)
        mask_u8 = raw_g[1][:].rearrange("p k i -> p (k i)").bitcast(U8)[:, 0:TB * S].rearrange("p (j s) -> p j s", j=TB)
        mask_add = sb("mask_add", [P, TB, S], BF16, a_mem)
        kpm_u8 = sb("kpm_u8", [P, S], U8, a_mem)
        kpm_add = sb("kpm_add", [P, S], BF16, a_mem)
        both_add = sb("both_add", [P, 2, S], BF16, a_mem)
        ctx_sb = [sb(f"ctx_sb{i}", [P, CC, S], F32, a_mem) for i in range(2)]
        qk = [sb(f"qk{i}", [P, 2, CC, S], F32, a_mem) for i in range(2)]
        xb = [sb(f"xb{i}", [P, H], F32, a_mem) for i in range(4)]
        junk = sb("junk", [P, S], BF16, a_mem)
        zb = [sb(f"zb{i}", [P, S], F32, a_mem) for i in range(2)]
        hT = sb("hT", [P, KH, P], F32, a_mem)
        hrow = [sb(f"hrow{i}", [P, HW], F32, a_mem) for i in range(4)]
        xsum = sb("xsum", [P, 4], F32, a_mem)
        nmean = sb("nmean", [P, 4], F32, a_mem)
        xssq = sb("xssq", [P, 4], F32, a_mem)
        sc = [sb(f"sc{i}", [P, 16], F32, a_mem) for i in range(2)]
        xscale = [sb(f"xscale{i}", [P, 1], F32, a_mem) for i in range(2)]
        half_pow = sb("half_pow", [P, 1], F32, a_mem)
        xvar = sb("xvar", [P, 1], F32, a_mem)
        norm = [sb(f"norm{i}", [P, 2], F32, a_mem) for i in range(2)]
        psum_p = sb("psum_p", [P, 2], F32, a_mem)
        bn = [sb(f"bn{i}", [P, 2, 6], F32, a_mem) for i in range(2)]
        lg = [sb(f"lg{i}", [P, E], F32, a_mem) for i in range(2)]
        top = [sb(f"top{i}", [P, TOPK], F32, a_mem) for i in range(2)]
        ntop = [sb(f"ntop{i}", [P, 1], F32, a_mem) for i in range(2)]
        left = sb("left", [P, E], F32, a_mem)
        sel = [sb(f"sel{i}", [P, E], BF16, a_mem) for i in range(2)]
        taken = [sb(f"taken{i}", [P, E], BF16, a_mem) for i in range(2)]
        e8 = sb("e8", [P, TOPK], F32, a_mem)
        e8sum = [sb(f"e8sum{i}", [P, 1], F32, a_mem) for i in range(2)]
        ew = [sb(f"ew{i}", [P, E], F32, a_mem) for i in range(2)]
        q_ = sb("q_", [P, E], F32, a_mem)
        fits = sb("fits", [P, E], F32, a_mem)
        place = sb("place", [P, E], F32, a_mem)
        key = sb("key", [P, E], F32, a_mem)
        key8 = sb("key8", [P, TOPK], F32, a_mem)
        r8 = sb("r8", [P, 2], F32, a_mem)
        a_mem.close()

        split_g = [sb(f"split_g{u}", [P, 2, KH, I], BF16) for u in range(2)]
        split_u = [sb(f"split_u{u}", [P, 2, KH, I], BF16) for u in range(2)]
        split_d = sb("split_d", [P, 2, MI, H], BF16)
        xg = [sb(f"xg{u}", [P, 2, HW], F32) for u in range(2)]
        xT = [sb(f"xT{u}", [P, KH, 2, CAP], BF16) for u in range(2)]
        g_idx = [sb(f"g_idx{u}", [P, 2], I32) for u in range(2)]
        s_idx = [sb(f"s_idx{u}", [P, 2], I32) for u in range(2)]
        wcol = [sb(f"wcol{u}", [P, 2], F32) for u in range(2)]
        sil = sb("sil", [P, MI, CAP], F32)
        prod = sb("prod", [P, MI, CAP], F32)
        act = [sb(f"act{u}", [P, 2, MI, CAP], BF16) for u in range(2)]
        ob = [sb(f"ob{u}", [P, 2, H], F32) for u in range(2)]

        consts_made = sem("consts_made")
        small_loaded = sem("small_loaded")
        mask_loaded = sem("mask_loaded")
        tanh_ready = sem("tanh_ready")
        rows_cleared = sem("rows_cleared")
        ctx_loaded = [sem(f"ctx_loaded{i}") for i in range(2)]
        kpm_loaded = sem("kpm_loaded")
        kpm_used = sem("kpm_used")
        mask_used = sem("mask_used")
        w_loaded = sem("w_loaded")
        proj_done = sem("proj_done")
        proj_out = sem("proj_out")
        scores_done = sem("scores_done")
        scores_used = sem("scores_used")
        x_loaded = [sem(f"x_loaded{i}") for i in range(4)]
        x_summed = sem("x_summed")
        nmean_ready = sem("nmean_ready")
        x_squared = sem("x_squared")
        z_ready = sem("z_ready")
        exp_done = sem("exp_done")
        x1_ready = sem("x1_ready")
        xscale_ready = sem("xscale_ready")
        var_ready = sem("var_ready")
        norm_ready = sem("norm_ready")
        h_done = sem("h_done")
        hT_done = sem("hT_done")
        hT_out = sem("hT_out")
        logits_done = sem("logits_done")
        chosen = sem("chosen")
        pos_done = sem("pos_done")
        ew_done = sem("ew_done")
        routed = sem("routed")
        x1_stored = [sem(f"x1_stored{i}") for i in range(4)]
        h_stored = [sem(f"h_stored{i}") for i in range(4)]
        places_stored = [sem(f"places_stored{i}") for i in range(2)]
        table_loaded = sem("table_loaded")
        dve_chain = sem("dve_chain")
        act_chain = sem("act_chain")
        pool_chain = sem("pool_chain")
        g_loaded = [sem(f"g_loaded{u}") for u in range(2)]
        u_loaded = [sem(f"u_loaded{u}") for u in range(2)]
        d_loaded = sem("d_loaded")
        g_high, g_low = sem("g_high"), sem("g_low")
        u_high, u_low = sem("u_high"), sem("u_low")
        d_high, d_low = sem("d_high"), sem("d_low")
        gathered = [sem(f"gathered{u}") for u in range(2)]
        wcol_ready = sem("wcol_ready")
        xT_done = sem("xT_done")
        xT_high = sem("xT_high")
        xT_out = sem("xT_out")
        gu_done = sem("gu_done")
        sil_done = sem("sil_done")
        act_ready = sem("act_ready")
        down_done = sem("down_done")
        down_out = sem("down_out")
        scattered = sem("scattered")

        CONSTS = 9
        SMALL = 3

        p_mem = ExitStack()
        ps = lambda name, shape, dt, where: where.enter_context(nc.psum_tensor(name, shape, dt))
        ps_s = [ps(f"ps_s{i}", [P, S], F32, p_mem) for i in range(2)]
        ps_t = ps("ps_t", [P, KH // 2, P], F32, p_mem)
        ps_j = ps("ps_j", [P, NH], F32, p_mem)
        ps_l = ps("ps_l", [P, NH], F32, p_mem)
        ps_p = ps("ps_p", [P, NH], F32, p_mem)
        p_mem.close()
        ps_gu = [ps(f"ps_gu{m}", [P, 2, CAP], F32, ctx) for m in range(MI)]
        ps_x = [ps(f"ps_x{i}", [P, 2, CAP], F32, ctx) for i in range(2)]
        ps_d = [ps(f"ps_d{i}", [P, NH], F32, ctx) for i in range(2)]

        block = ctx.enter_context(nc.Block())

        CHUNKS = [(1, 0, 0), (1, 0, 1), (1, 1, 0), (1, 1, 1), (0, 0, 0), (0, 1, 0), (0, 0, 1), (0, 1, 1)]

        def attention_done(eng):
            eng.wait_ge(routed, N)
            for i in range(4):
                eng.wait_ge(x1_stored[i], 16 * N // 4)
                eng.wait_ge(h_stored[i], 16 * N // 4)

        @block.sync
        def _(sp):
            def load_ctx(b):
                sp.dma_start(ctx_sb[b % 2][:], ctxT[b]).then_inc(ctx_loaded[b % 2], 16)

            def load_kpm(b):
                sp.dma_start(kpm_u8[:], kpm[b].partition_broadcast(P)).then_inc(kpm_loaded, 16)

            def load_x(g):
                sp.dma_start(xb[g % 4][:], x[g * P:(g + 1) * P, :]).then_inc(x_loaded[g % 4], 16)

            def load_expert(e, u):
                sp.dma_start(raw_g[u][:], wg[bass.ds(e, 1)].rearrange("e p k i -> p (e k) i")).then_inc(g_loaded[u], 16)
                sp.dma_start(raw_u[u][:], wu[bass.ds(e, 1)].rearrange("e p k i -> p (e k) i")).then_inc(u_loaded[u], 16)

            def load_down(e):
                sp.dma_start(raw_d[:], wd[bass.ds(e, 1)].rearrange("e p m h -> p (e m) h")).then_inc(d_loaded, 16)

            def store_h(g):
                sp.wait_ge(routed, g + 1)
                sp.dma_start(h_rows[g * P:(g + 1) * P, :], hrow[g % 4][:]).then_inc(h_stored[g % 4], 16)

            sp.dma_start(w_qk[:, 1], wkT).then_inc(w_loaded, 16)
            sp.dma_start(b_qk[:, 1], bkT).then_inc(w_loaded, 16)
            load_ctx(0)
            sp.dma_start(w_qk[:, 0], wqT).then_inc(w_loaded, 16)
            sp.dma_start(b_qk[:, 0], bqT).then_inc(w_loaded, 16)
            load_x(0)
            sp.dma_start(gates[:, 0:1], g_x.partition_broadcast(P)).then_inc(small_loaded, 16)
            sp.dma_start(gates[:, 1:2], g_f.partition_broadcast(P)).then_inc(small_loaded, 16)
            load_kpm(0)
            sp.dma_start(mask_u8, mask.rearrange("(j p) s -> p j s", p=P)).then_inc(mask_loaded, 16)
            load_x(1)
            sp.dma_start(gw_sb[:], gwT).then_inc(small_loaded, 16)
            load_x(2)
            load_ctx(1)
            sp.wait_ge(consts_made, CONSTS)
            for half in range(2):
                r = slice(T + half * P, T + (half + 1) * P)
                sp.dma_start(h_rows[r, :], hrow[3][:]).then_inc(rows_cleared, 16)
                sp.dma_start(out[r, :], hrow[3][:, 0:H]).then_inc(rows_cleared, 16)
            sp.dma_start(place_table.rearrange("(p k) o -> p (k o)", p=P),
                         free_rows[:].rearrange("p t e -> p (t e)")).then_inc(rows_cleared, 16)
            load_expert(0, 0)
            load_down(0)
            sp.wait_ge(mask_used, TB)
            load_expert(1, 1)

            for g in range(N):
                b, j = g // TB, g % TB
                sp.wait_ge(x1_ready, g + 1)
                sp.dma_start(out[g * P:(g + 1) * P, :], xb[g % 4][:]).then_inc(x1_stored[g % 4], 16)
                if g >= 2:
                    store_h(g - 2)
                if g + 3 < N:
                    if g >= 1:
                        sp.wait_ge(x1_stored[(g - 1) % 4], 16 * ((g - 1) // 4 + 1))
                        sp.wait_ge(h_done, g)
                    load_x(g + 3)
                if j == 0 and b < B - 2:
                    sp.wait_ge(proj_done, 8 * (b + 1))
                    load_ctx(b + 2)
                if j == 0 and b < B - 1:
                    sp.wait_ge(kpm_used, b + 1)
                    load_kpm(b + 1)
            for g in (N - 2, N - 1):
                store_h(g)
            for i in range(2):
                sp.wait_ge(places_stored[i], 16 * TOPK * N // 2)
            sp.dma_start(table[:].rearrange("p t e -> p (t e)"),
                         place_table.rearrange("(p k) o -> p (k o)", p=P)).then_inc(table_loaded, 16)

            def expert(e, u, ahead):
                if ahead >= 1:
                    sp.wait_ge(d_low, 2 * e + 2)
                    load_down(e + 1)
                if ahead >= 2:
                    sp.wait_ge(g_low, 2 * e + 2)
                    sp.wait_ge(u_low, 2 * e + 2)
                    load_expert(e + 2, u)

            with sp.Fori(0, E // 2 - 1) as i:
                expert(2 * i, 0, 2)
                expert(2 * i + 1, 1, 2)
            expert(E - 2, 0, 1)
            sp.wait_ge(scattered, 32 * E)

        @block.tensor
        def _(pe):
            def project(b, i):
                which, o, n = CHUNKS[i]
                bank = ps_t[:].rearrange("p k t -> p (k t)") if b == 0 and i % 2 else ps_j[:]
                pe.wait_ge(ctx_loaded[b % 2], 16 * (b // 2 + 1))
                behind = 8 * b + i - (1 if b == 0 else 0)
                if behind > 0:
                    pe.wait_ge(proj_out, behind)
                for k in range(CC):
                    mm = pe.matmul(bank, w_qk[:, which, k, o * P:(o + 1) * P], ctx_sb[b % 2][:, k, n * NH:(n + 1) * NH],
                                   start=(k == 0), stop=(k == CC - 1))
                mm.then_inc(proj_done, 1)

            def scores(g):
                b, j = g // TB, g % TB
                pe.wait_ge(proj_out, 8 * b + (6 if j < TB // 2 else 8))
                if g >= 2:
                    pe.wait_ge(scores_used, g - 1)
                for n in range(S // NH):
                    for k in range(CC):
                        mm = pe.matmul(ps_s[g % 2][:, n * NH:(n + 1) * NH], qk[b % 2][:, 0, k, j * P:(j + 1) * P],
                                       qk[b % 2][:, 1, k, n * NH:(n + 1) * NH], start=(k == 0), stop=(k == CC - 1))
                mm.then_inc(scores_done, 1)

            def turn_h(g, half):
                pe.wait_ge(h_done, g + 1)
                if g or half:
                    pe.wait_ge(hT_out, 2 * g + half)
                for k in range(KH // 2):
                    at = (half * KH // 2 + k) * P
                    mm = pe.transpose(ps_t[:, k, :], hrow[g % 4][:, at:at + P], ident[:])
                mm.then_inc(hT_done, 1)

            def logits(g):
                pe.wait_ge(hT_out, 2 * g + 2)
                if g:
                    pe.wait_ge(chosen, g)
                for k in range(KH):
                    mm = pe.matmul(ps_l[:, 0:E], hT[:, k, :], gw_sb[:, k, :], start=(k == 0), stop=(k == KH - 1))
                mm.then_inc(logits_done, 1)

            def positions(g):
                pe.wait_ge(chosen, g + 1)
                if g:
                    pe.wait_ge(routed, g)
                pe.matmul(ps_p[:, 0:E], before[:], sel[g % 2][:], start=True, stop=False)
                pe.matmul(ps_p[:, 0:E], ones[:], taken[g % 2][:], start=False, stop=True).then_inc(pos_done, 1)

            pe.wait_ge(w_loaded, 16 * 4)
            for i in range(6):
                project(0, i)
            scores(0)
            for i in range(6, 8):
                project(0, i)
            pe.wait_ge(small_loaded, 16 * SMALL)
            pe.wait_ge(consts_made, CONSTS)
            for g in range(N + 1):
                if g >= 1:
                    turn_h(g - 1, 0)
                if g + TB < N:
                    project(g // TB + 1, g % TB)
                if g >= 1:
                    turn_h(g - 1, 1)
                    logits(g - 1)
                if g + 1 < N:
                    scores(g + 1)
                if g >= 1:
                    positions(g - 1)

            def turn(e, u, q, first=False):
                pe.wait_ge(gathered[u], 16 * (e - u) + 32)
                if not (first and q < 2):
                    pe.wait_ge(xT_out, 4 * e + q - 1)
                for kk in range(2):
                    for half in range(2):
                        at = (2 * q + kk) * P
                        mm = pe.transpose(ps_x[q % 2][:, kk, half * P:(half + 1) * P], xg[u][:, half, at:at + P], ident[:])
                mm.then_inc(xT_done, 1)

            PAIRS = ((0, 0), (0, 1), (1, 0))

            def gate_up(e, u, m, first=False):
                if m == 0:
                    pe.wait_ge(xT_out, 4 * e + 4)
                if not first:
                    pe.wait_ge(act_ready, MI * e - MI + m + 1)
                for t, w in ((0, split_g[u]), (1, split_u[u])):
                    if m == 0:
                        pe.wait_ge((g_low, u_low)[t], 2 * e + 2)
                    for k in range(KH):
                        for wi, xi in PAIRS:
                            mm = pe.matmul(ps_gu[m][:, t, :], w[:, wi, k, m * P:(m + 1) * P], xT[u][:, k, xi, :],
                                           start=(k == 0 and (wi, xi) == (0, 0)),
                                           stop=(k == KH - 1 and (wi, xi) == (1, 0)))
                mm.then_inc(gu_done, 1)

            def down_part(u, n, ms):
                half, c = n // 2, n % 2
                for m in ms:
                    for wi, ai in PAIRS:
                        mm = pe.matmul(ps_d[n % 2][:], act[u][:, ai, m, half * P:(half + 1) * P],
                                       split_d[:, wi, m, c * NH:(c + 1) * NH],
                                       start=(m == 0 and (wi, ai) == (0, 0)),
                                       stop=(m == MI - 1 and (wi, ai) == (1, 0)))
                return mm

            def down(e, u, first=False):
                pe.wait_ge(d_low, 2 * e + 2)
                pe.wait_ge(act_ready, MI * e + MI - 1)
                for n in range(2):
                    if not first:
                        pe.wait_ge(down_out, 4 * e + n - 1)
                    down_part(u, n, range(MI - 1))
                pe.wait_ge(act_ready, MI * e + MI)
                for n in range(2):
                    down_part(u, n, [MI - 1]).then_inc(down_done, 1)
                for n in range(2, 4):
                    pe.wait_ge(down_out, 4 * e + n - 1)
                    down_part(u, n, range(MI)).then_inc(down_done, 1)

            def expert(e, u, first=False, last=False):
                for m in range(MI):
                    gate_up(e, u, m, first)
                    if m < 2 and not last:
                        turn(e + 1, 1 - u, 2 * m)
                        turn(e + 1, 1 - u, 2 * m + 1)
                down(e, u, first)

            attention_done(pe)
            for q in range(4):
                turn(0, 0, q, True)
            expert(0, 0, True)
            with pe.Fori(0, E // 2 - 1) as i:
                expert(2 * i + 1, 1)
                expert(2 * i + 2, 0)
            expert(E - 1, 1, False, True)

        @block.scalar
        def _(s):
            s.wait_ge(w_loaded, 16 * 4)

            def project_out(b, i):
                which, o, n = CHUNKS[i]
                bank = ps_t[:].rearrange("p k t -> p (k t)") if b == 0 and i % 2 else ps_j[:]
                s.wait_ge(proj_done, 8 * b + i + 1)
                if b >= 2 and i == 0:
                    s.wait_ge(scores_done, (b - 1) * TB)
                s.activation(qk[b % 2][:, which, o, n * NH:(n + 1) * NH], bank, ACT.Identity,
                             bias=b_qk[:, which, o:o + 1]).then_inc(proj_out, 1)

            def x_sum(g):
                s.wait_ge(x_loaded[g % 4], 16 * (g // 4 + 1))
                if g == 1:
                    s.wait_ge(x_summed, 1)
                if g >= 2:
                    s.wait_ge(x_squared, g)
                s.activation(junk[:], xb[g % 4][:], ACT.Identity, accum_out=xsum[:, g % 4:g % 4 + 1]).then_inc(x_summed, 1)

            def x_square(g):
                s.wait_ge(nmean_ready, g + 1)
                s.wait_ge(x_summed, max(g + 1, 2))
                s.activation(junk[:], xb[g % 4][:], ACT.Square, bias=nmean[:, g % 4:g % 4 + 1],
                             accum_out=xssq[:, g % 4:g % 4 + 1]).then_inc(x_squared, 1)

            def softmax(g):
                s.wait_ge(z_ready, g + 1)
                s.activation(zb[g % 2][:], zb[g % 2][:], ACT.Exp, bias=sc[g % 2][:, 2:3], scale=xscale[g % 2][:],
                             accum_out=psum_p[:, g % 2:g % 2 + 1]).then_inc(exp_done, 1)

            def normalize(g):
                s.wait_ge(norm_ready, g + 1)
                if g == 3:
                    s.wait_ge(rows_cleared, 16 * 5)
                if g >= 4:
                    s.wait_ge(h_stored[g % 4], 16 * (g // 4))
                s.activation(hrow[g % 4][:, 0:H], xb[g % 4][:], ACT.Identity, bias=norm[g % 2][:, 1:2],
                             scale=norm[g % 2][:, 0:1]).then_inc(h_done, 1)

            def turned_out(g, half):
                s.wait_ge(hT_done, 2 * g + half + 1)
                if g:
                    s.wait_ge(logits_done, g)
                s.activation(hT[:, half * KH // 2:(half + 1) * KH // 2], ps_t[:], ACT.Copy).then_inc(hT_out, 1)

            def expert_weights(g):
                u = g % 2
                s.wait_ge(chosen, g + 1)
                if g:
                    s.wait_ge(ew_done, g)
                s.activation(e8[:], top[u][:], ACT.Exp, bias=ntop[u][:], accum_out=e8sum[u][:])
                s.activation(ew[u][:], lg[u][:], ACT.Exp, bias=ntop[u][:]).then_inc(ew_done, 1)

            for i in range(6):
                project_out(0, i)
            x_sum(0)
            x_sum(1)
            x_square(0)
            for i in range(6, 8):
                project_out(0, i)
            s.wait_ge(small_loaded, 16 * SMALL)
            s.activation(tanh_g[:], gates[:], ACT.Tanh).then_inc(tanh_ready, 1)
            for g in range(N + 2):
                if 1 <= g <= N:
                    turned_out(g - 1, 0)
                if g + TB < N:
                    project_out(g // TB + 1, g % TB)
                if 1 <= g <= N:
                    turned_out(g - 1, 1)
                if g >= 2:
                    expert_weights(g - 2)
                if g < N:
                    softmax(g)
                if g + 1 < N:
                    x_square(g + 1)
                if g + 2 < N:
                    x_sum(g + 2)
                if g < N:
                    normalize(g)

            attention_done(s)

            def gate_high(e, u, part, first=False):
                s.wait_ge(g_loaded[u], 8 * (e - u) + 16)
                if not first:
                    s.wait_ge(gu_done, MI * e - MI)
                ks = slice(part * KH // 2, (part + 1) * KH // 2)
                s.activation(split_g[u][:, 0, ks], raw_g[u][:, ks], ACT.Copy).then_inc(g_high, 1)

            def up_high(e, u, part, first=False):
                s.wait_ge(u_loaded[u], 8 * (e - u) + 16)
                if not first:
                    s.wait_ge(gu_done, MI * e - MI)
                ks = slice(part * KH // 2, (part + 1) * KH // 2)
                s.activation(split_u[u][:, 0, ks], raw_u[u][:, ks], ACT.Copy).then_inc(u_high, 1)

            def down_high(e, part, first=False):
                s.wait_ge(d_loaded, 16 * e + 16)
                if not first:
                    s.wait_ge(down_done, 4 * e)
                cs = slice(part * NH, (part + 1) * NH)
                s.activation(split_d[:, 0, :, cs], raw_d[:, :, cs], ACT.Copy).then_inc(d_high, 1)

            def silu(e, m):
                s.wait_ge(gu_done, MI * e + m + 1)
                s.activation(sil[:, m], ps_gu[m][:, 0], ACT.Silu).then_inc(sil_done, 1)

            def turned_high(e, u, q):
                s.wait_ge(xT_done, 4 * e + q + 1)
                s.activation(xT[u][:, 2 * q:2 * q + 2, 0], ps_x[q % 2][:], ACT.Copy).then_inc(xT_high, 1)

            def rows_out(e, u, first=False):
                s.wait_ge(wcol_ready, e + 1)
                if not first:
                    s.wait_ge(scattered, 32 * e - 32)
                for n in range(4):
                    s.wait_ge(down_done, 4 * e + n + 1)
                    s.activation(ob[u][:, n // 2, n % 2 * NH:(n % 2 + 1) * NH], ps_d[n % 2][:], ACT.Copy,
                                 scale=wcol[u][:, n // 2:n // 2 + 1]).then_inc(down_out, 1)

            def expert(e, u, first=False, last=False):
                none_before = first and u == 0
                down_high(e, 0, none_before)
                down_high(e, 1, none_before)
                silu(e, 0)
                if not last:
                    turned_high(e + 1, 1 - u, 0)
                    turned_high(e + 1, 1 - u, 1)
                    gate_high(e + 1, 1 - u, 0, none_before)
                    gate_high(e + 1, 1 - u, 1, none_before)
                silu(e, 1)
                if not last:
                    turned_high(e + 1, 1 - u, 2)
                    turned_high(e + 1, 1 - u, 3)
                    up_high(e + 1, 1 - u, 0, none_before)
                silu(e, 2)
                if not last:
                    up_high(e + 1, 1 - u, 1, none_before)
                rows_out(e, u, first)

            for part in range(2):
                gate_high(0, 0, part, True)
            for part in range(2):
                up_high(0, 0, part, True)
            for q in range(4):
                turned_high(0, 0, q)
            expert(0, 0, True)
            expert(1, 1, True)
            with s.Fori(1, E // 2 - 1) as i:
                expert(2 * i, 0)
                expert(2 * i + 1, 1)
            expert(E - 2, 0)
            expert(E - 1, 1, False, True)

        @block.vector
        def _(v):
            chain = Chain(v, dve_chain)

            def minus_mean(g):
                v.wait_ge(x_summed, g + 1)
                v.tensor_scalar(nmean[:, g % 4:g % 4 + 1], xsum[:, g % 4:g % 4 + 1], -1.0 / H, None,
                                ALU.mult).then_inc(nmean_ready, 1)

            def key_mask(b):
                v.wait_ge(kpm_loaded, 16 * (b + 1))
                v.tensor_scalar(kpm_add[:], kpm_u8[:], MASKED, None, ALU.mult).then_inc(kpm_used, 1)

            def both(g):
                v.wait_ge(kpm_used, g // TB + 1)
                return chain.mark(v.tensor_tensor(both_add[:, g % 2], mask_add[:, g % TB], kpm_add[:], ALU.add))

            def route(g):
                u = g % 2
                v.wait_ge(pos_done, g + 1)
                t = chain.mark(v.scalar_tensor_tensor(q_[:], sel[u][:], -BIG, ps_p[:, 0:E], ALU.mult, ALU.add))
                yield
                chain.wait(t)
                v.tensor_scalar(fits[:], q_[:], CAP - BIG, None, ALU.is_lt)
                t = chain.mark(v.scalar_tensor_tensor(place[:], q_[:], float(E), expert_no[:], ALU.mult, ALU.add))
                yield
                chain.wait(t)
                t = chain.mark(v.scalar_tensor_tensor(key[:], place[:], -1.0, fits[:], ALU.mult, ALU.mult))
                v.wait_ge(ew_done, g + 1)
                r = chain.mark(v.reciprocal(r8[:, 0:1], e8sum[u][:]))
                yield
                chain.wait(t)
                t = chain.mark(v.max(key8[:], key[:]))
                chain.wait(r)
                r = chain.mark(v.tensor_tensor(r8[:, 1:2], r8[:, 0:1], tanh_g[:, 1:2], ALU.mult))
                yield
                if g >= 2:
                    v.wait_ge(places_stored[u], 16 * TOPK * (g // 2))
                chain.wait(r)
                chain.mark(v.tensor_scalar(where8[u][:], key8[:], -1.0, KEY0, ALU.mult, ALU.add))
                v.scalar_tensor_tensor(hrow[g % 4][:, H:HW], ew[u][:], r8[:, 1:2], fits[:], ALU.mult,
                                       ALU.mult).then_inc(routed, 1)
                yield

            def choose(g):
                u = g % 2
                v.wait_ge(logits_done, g + 1)
                if g >= 2:
                    v.wait_ge(ew_done, g - 1)
                t = chain.mark(v.tensor_copy(lg[u][:], ps_l[:, 0:E]))
                yield
                chain.wait(t)
                t = chain.mark(v.max(top[u][:], lg[u][:]))
                yield
                chain.wait(t)
                t = chain.mark(v.match_replace(left[:], top[u][:], lg[u][:], -3.0e38))
                v.tensor_scalar(ntop[u][:], top[u][:, 0:1], -1.0, None, ALU.mult)
                yield
                chain.wait(t)
                if g >= 1:
                    v.wait_ge(pos_done, g)
                t = chain.mark(v.tensor_scalar(sel[u][:], left[:], -3.0e38, None, ALU.is_le))
                yield
                chain.wait(t)
                v.tensor_tensor(taken[1 - u][:], taken[u][:], sel[u][:], ALU.add).then_inc(chosen, 1)
                yield

            v.wait_ge(mask_loaded, 16)
            for j in range(TB):
                v.tensor_scalar(mask_add[:, j], mask_u8[:, j], MASKED, None, ALU.mult).then_inc(mask_used, 1)
            chain.mark(v.memset(taken[0][:], 0.0))
            key_mask(0)
            v.wait_ge(mask_used, TB)
            both_made = both(0)
            minus_mean(0)
            minus_mean(1)
            v.wait_ge(tanh_ready, 1)
            v.wait_ge(consts_made, CONSTS)
            for g in range(N):
                u, f = g % 2, g % 4
                c = sc[u]
                older = route(g - 2) if g >= 2 else iter(())
                newer = choose(g - 1) if g >= 1 else iter(())
                v.wait_ge(nmean_ready, g + 1)
                v.wait_ge(x_squared, g + 1)
                v.wait_ge(scores_done, g + 1)
                v.scalar_tensor_tensor(zb[u][:], xb[f][:], nmean[:, f:f + 1], ps_s[u][:], ALU.add, ALU.mult
                                       ).then_inc(scores_used, 1)
                next(older, None)
                v.wait_ge(scores_used, g + 1)
                chain.wait(both_made)
                t = chain.mark(v.tensor_tensor_reduce(zb[u][:], zb[u][:], both_add[:, u], 1.0, -3.0e38, ALU.add,
                                                      ALU.max, c[:, 3:4]))
                next(older, None)
                chain.wait(t)
                v.wait_ge(xscale_ready, g + 1)
                v.scalar_tensor_tensor(c[:, 2:3], c[:, 3:4], -1.0, xscale[u][:], ALU.mult, ALU.mult).then_inc(z_ready, 1)
                next(older, None)
                if g + 1 < N:
                    if (g + 1) % TB == 0:
                        key_mask((g + 1) // TB)
                    both_made = both(g + 1)
                next(older, None)
                next(older, None)
                v.wait_ge(exp_done, g + 1)
                chain.link(v.reciprocal(c[:, 4:5], psum_p[:, u:u + 1]))
                chain.link(v.tensor_tensor(c[:, 5:6], c[:, 4:5], tanh_g[:, 0:1], ALU.mult))
                v.scalar_tensor_tensor(xb[f][:], zb[u][:], c[:, 5:6], xb[f][:], ALU.mult, ALU.add).then_inc(x1_ready, 1)
                next(newer, None)
                v.wait_ge(x1_ready, g + 1)
                v.bn_stats(bn[u][:, 0], xb[f][:, 0:NH])
                next(newer, None)
                t = chain.mark(v.bn_stats(bn[u][:, 1], xb[f][:, NH:2 * NH]))
                next(newer, None)
                chain.wait(t)
                t = chain.mark(v.bn_aggr(c[:, 10:12], bn[u][:].rearrange("p a b -> p (a b)")))
                next(newer, None)
                chain.wait(t)
                if g >= 2:
                    v.wait_ge(norm_ready, g - 1)
                v.tensor_scalar(c[:, 9:10], c[:, 10:11], -1.0, None, ALU.mult)
                v.tensor_scalar(c[:, 6:7], c[:, 11:12], LN_EPS, None, ALU.add).then_inc(var_ready, 1)
                next(newer, None)
                if g + 2 < N:
                    minus_mean(g + 2)
            for steps in (route(N - 2), choose(N - 1), route(N - 1)):
                for _ in steps:
                    pass


            attention_done(v)

            def gate_low(e, u, part):
                v.wait_ge(g_high, 2 * e + part + 1)
                ks = slice(part * KH // 2, (part + 1) * KH // 2)
                v.tensor_tensor(split_g[u][:, 1, ks], raw_g[u][:, ks], split_g[u][:, 0, ks], ALU.subtract).then_inc(g_low, 1)

            def up_low(e, u, part):
                v.wait_ge(u_high, 2 * e + part + 1)
                ks = slice(part * KH // 2, (part + 1) * KH // 2)
                v.tensor_tensor(split_u[u][:, 1, ks], raw_u[u][:, ks], split_u[u][:, 0, ks], ALU.subtract).then_inc(u_low, 1)

            def down_low(e, part):
                v.wait_ge(d_high, 2 * e + part + 1)
                cs = slice(part * NH, (part + 1) * NH)
                v.tensor_tensor(split_d[:, 1, :, cs], raw_d[:, :, cs], split_d[:, 0, :, cs], ALU.subtract
                                ).then_inc(d_low, 1)

            def activate(e, u, m, first):
                v.wait_ge(sil_done, MI * e + m + 1)
                if m == 0 and not first:
                    v.wait_ge(down_done, 4 * e - 4)
                chain.link(v.tensor_tensor(prod[:, m], sil[:, m], ps_gu[m][:, 1], ALU.mult))
                chain.link(v.tensor_copy(act[u][:, 0, m], prod[:, m]))
                v.tensor_tensor(act[u][:, 1, m], prod[:, m], act[u][:, 0, m], ALU.subtract).then_inc(act_ready, 1)

            def turned_low(e, u, q):
                v.wait_ge(xT_high, 4 * e + q + 1)
                v.tensor_tensor(xT[u][:, 2 * q:2 * q + 2, 1], ps_x[q % 2][:], xT[u][:, 2 * q:2 * q + 2, 0], ALU.subtract
                                ).then_inc(xT_out, 1)

            def expert(e, u, first=False, last=False):
                down_low(e, 0)
                down_low(e, 1)
                activate(e, u, 0, first)
                if not last:
                    turned_low(e + 1, 1 - u, 0)
                    turned_low(e + 1, 1 - u, 1)
                    gate_low(e + 1, 1 - u, 0)
                    gate_low(e + 1, 1 - u, 1)
                activate(e, u, 1, first)
                if not last:
                    turned_low(e + 1, 1 - u, 2)
                    turned_low(e + 1, 1 - u, 3)
                    up_low(e + 1, 1 - u, 0)
                activate(e, u, 2, first)
                if not last:
                    up_low(e + 1, 1 - u, 1)

            for part in range(2):
                gate_low(0, 0, part)
            for part in range(2):
                up_low(0, 0, part)
            for q in range(4):
                turned_low(0, 0, q)
            expert(0, 0, True)
            expert(1, 1, True)
            with v.Fori(1, E // 2 - 1) as i:
                chain.enter(i - 1, 12)
                expert(2 * i, 0)
                expert(2 * i + 1, 1)
                chain.leave(E // 2 - 2, 12)
            expert(E - 2, 0)
            expert(E - 1, 1, False, True)

        @block.gpsimd
        def _(p):
            chain = Chain(p, pool_chain)
            p.memset(ones[:], 1.0).then_inc(consts_made, 1)
            p.memset(half_pow[:], -0.5).then_inc(consts_made, 1)
            p.memset(ident[:], 0.0)
            made = chain.mark(p.memset(before[:], 1.0))
            p.memset(hrow[3][:], 0.0).then_inc(consts_made, 1)
            p.iota(free_rows[:], pattern=[[1, 2], [0, E]], base=T, channel_multiplier=2).then_inc(consts_made, 1)
            p.iota(token_no[:, 0:1], pattern=[[0, 1]], base=0, channel_multiplier=1).then_inc(consts_made, 1)
            p.iota(token_no[:, 1:2], pattern=[[0, 1]], base=P, channel_multiplier=1).then_inc(consts_made, 1)
            p.iota(expert_no[:], pattern=[[1, E]], base=0, channel_multiplier=0,
                   allow_small_or_imprecise_dtypes=True).then_inc(consts_made, 1)
            chain.wait(made)
            p.affine_select(out=ident[:], in_=ident[:], compare_op=ALU.not_equal, fill=1.0, base=0,
                            pattern=[[-1, P]], channel_multiplier=1).then_inc(consts_made, 1)
            p.affine_select(out=before[:], in_=before[:], compare_op=ALU.is_gt, fill=0.0, base=0,
                            pattern=[[1, P]], channel_multiplier=-1).then_inc(consts_made, 1)

            def x_scale(g):
                p.wait_ge(x_squared, g + 1)
                if g >= 2:
                    p.wait_ge(exp_done, g - 1)
                chain.link(p.tensor_scalar(xvar[:], xssq[:, g % 4:g % 4 + 1], D / H, D * LN_EPS, ALU.mult, ALU.add))
                p.tensor_tensor(xscale[g % 2][:], xvar[:], half_pow[:], ALU.pow).then_inc(xscale_ready, 1)

            def x1_norm(g):
                u = g % 2
                p.wait_ge(var_ready, g + 1)
                if g >= 2:
                    p.wait_ge(h_done, g - 1)
                chain.link(p.tensor_tensor(norm[u][:, 0:1], sc[u][:, 6:7], half_pow[:], ALU.pow))
                p.tensor_tensor(norm[u][:, 1:2], sc[u][:, 9:10], norm[u][:, 0:1], ALU.mult).then_inc(norm_ready, 1)

            def scatter_places(g, ks):
                u = g % 2
                p.wait_ge(routed, g + 1)
                for k in ks:
                    p.indirect_dma_start(
                        out=place_table, out_offset=bass.IndirectOffsetOnAxis(ap=where8[u][:, k:k + 1].bitcast(U32), axis=0),
                        in_=token_no[:, u:u + 1], in_offset=None, bounds_check=CAP * E - 1, oob_is_err=False,
                    ).then_inc(places_stored[u], 16)

            def next_tokens(g):
                u = g % 2
                p.wait_ge(places_stored[u], 16 * TOPK * (g // 2 + 1))
                chain.link(p.tensor_scalar(token_no[:, u:u + 1], token_no[:, u:u + 1], 2 * P, None, ALU.add))

            p.wait_ge(consts_made, CONSTS)
            x_scale(0)
            p.wait_ge(rows_cleared, 16 * 5)
            for g in range(N + 2):
                if g >= 4:
                    next_tokens(g - 4)
                if g >= 2:
                    scatter_places(g - 2, range(TOPK // 2))
                if g + 1 < N:
                    x_scale(g + 1)
                if g < N:
                    x1_norm(g)
                if g >= 2:
                    scatter_places(g - 2, range(TOPK // 2, TOPK))

            attention_done(p)
            for i in range(2):
                p.wait_ge(places_stored[i], 16 * TOPK * N // 2)
            p.wait_ge(table_loaded, 16)

            last_row = p.alloc_register("last_row")
            p.reg_mov(last_row, ROWS - 1)

            def hold():
                p.reg_alu(last_row, last_row, ROWS - 1, op=ALU.min)

            def gather(e, u):
                chain.link(p.tensor_copy(g_idx[u][:], table[:, :, bass.ds(e, 1)].rearrange("p t e -> p (t e)")))
                hold()
                for half in range(2):
                    p.indirect_dma_start(
                        out=xg[u][:, half, :], out_offset=None, in_=h_rows,
                        in_offset=bass.IndirectOffsetOnAxis(ap=g_idx[u][:, half:half + 1].bitcast(U32), axis=0),
                        bounds_check=last_row, oob_is_err=True,
                    ).then_inc(gathered[u], 16)

            def weights(e, u, first=False):
                p.wait_ge(gathered[u], 16 * (e - u) + 32)
                if not first:
                    p.wait_ge(down_out, 4 * e - 4)
                    p.wait_ge(scattered, 32 * e - 32)
                p.tensor_copy(wcol[u][:], xg[u][:, :, bass.ds(e + H, 1)].rearrange("p t e -> p (t e)")
                              ).then_inc(wcol_ready, 1)
                chain.link(p.tensor_copy(s_idx[u][:], g_idx[u][:]))

            def add_rows(e, u, first=False):
                p.wait_ge(down_out, 4 * e + 4)
                if not first:
                    p.wait_ge(scattered, 32 * e)
                hold()
                for half in range(2):
                    p.indirect_dma_start(
                        out=out, out_offset=bass.IndirectOffsetOnAxis(ap=s_idx[u][:, half:half + 1].bitcast(U32), axis=0),
                        in_=ob[u][:, half, :], in_offset=None, bounds_check=last_row, oob_is_err=True,
                        compute_op=ALU.add,
                    ).then_inc(scattered, 16)

            def expert(e, u, first=0, ahead=2):
                if ahead >= 2:
                    p.wait_ge(xT_done, 4 * e + 4)
                    p.wait_ge(wcol_ready, e + 1)
                    gather(e + 2, u)
                if ahead >= 1:
                    weights(e + 1, 1 - u, first == 1)
                add_rows(e, u, first == 1)

            gather(0, 0)
            gather(1, 1)
            weights(0, 0, True)
            expert(0, 0, 1)
            expert(1, 1)
            with p.Fori(1, E // 2 - 1) as i:
                chain.enter(i - 1, 4)
                expert(2 * i, 0)
                expert(2 * i + 1, 1)
                chain.leave(E // 2 - 2, 4)
            expert(E - 2, 0, 0, 1)
            expert(E - 1, 1, 0, 0)


def kernel(**inputs):
    import concourse.bacc as bacc
    from concourse.bass_utils import run_bass_kernel_spmd

    a = {k: np.asarray(v) for k, v in inputs.items()}
    B, S, H = a["x"].shape
    E, _, I = a["L0_ffn_wg"].shape
    D = a["ctx_512"].shape[2]

    def tiles(w, axis):
        shape = w.shape[:axis] + (w.shape[axis] // P, P) + w.shape[axis + 1:]
        return w.reshape(shape).swapaxes(axis, axis + 1)

    arrays = {
        "x": a["x"].reshape(B * S, H),
        "ctxT": tiles(a["ctx_512"].transpose(0, 2, 1), 1),
        "mask": a["mask_SxS2_bk1"],
        "kpm": a["mask_BxS2_bf0"],
        "g_x": a["g_xattn"], "g_f": a["g_ffn"],
        "wqT": tiles(a["L0_xattn_Wq"].T, 0), "bqT": tiles(a["L0_xattn_bq"], 0),
        "wkT": tiles(a["L0_xattn_Wk"].T, 0), "bkT": tiles(a["L0_xattn_bk"], 0),
        "gwT": tiles(a["L0_ffn_gate_w"].T, 0),
        "wg": tiles(a["L0_ffn_wg"], 1), "wu": tiles(a["L0_ffn_wu"], 1), "wd": tiles(a["L0_ffn_wd"], 1),
    }
    nc = bacc.Bacc("TRN2", target_bir_lowering=False, num_devices=1)
    sent, aps = {}, []
    for name, v in arrays.items():
        v = np.ascontiguousarray(v)
        sent[f"in_{name}"] = v
        aps.append(nc.dram_tensor(f"in_{name}", v.shape, mybir.dt.from_np(v.dtype), kind="ExternalInput").ap())
    out = nc.dram_tensor("out", (B * S + CAP, H), F32, kind="ExternalOutput").ap()
    flamingo_moe(nc, *aps, out)
    r = run_bass_kernel_spmd(nc, [sent], core_ids=[0])
    return r.results[0]["out"][:B * S].reshape(B, S, H)
```

```python
from contextlib import ExitStack

import numpy as np

import concourse.bass as bass
from concourse import mybir

P = 128
ALU = mybir.AluOpType
ACT = mybir.ActivationFunctionType
F32 = mybir.dt.float32
BF16 = mybir.dt.bfloat16
I32 = mybir.dt.int32
U32 = mybir.dt.uint32
U8 = mybir.dt.uint8

MASKED = -1.0e30
LN_EPS = 1.0e-5
CAP = 256
TOPK = 8


class Chain:

    def __init__(self, eng, sem):
        self.eng, self.sem, self.base, self.n = eng, sem, 0, 0

    def mark(self, ins):
        ins.then_inc(self.sem, 1)
        self.n += 1
        return self.base + self.n

    def wait(self, value):
        self.eng.wait_ge(self.sem, value)

    def link(self, ins):
        self.wait(self.mark(ins))

    def enter(self, passes_before, per_pass):
        self.start = self.base + self.n
        self.base, self.n = self.start + passes_before * per_pass, 0

    def leave(self, passes, per_pass):
        assert self.n == per_pass, (self.n, per_pass)
        self.base, self.n = self.start + passes * per_pass, 0


def flamingo_moe(nc, x, ctxT, mask, kpm, g_x, g_f, wqT, bqT, wkT, bkT, gwT, wg, wu, wd, out):
    B, CP, CC, S = ctxT.shape
    T, H = x.shape
    E, _, KH, I = wg.shape
    MI = I // P
    TB = S // P
    NH = 512
    D = CC * P
    HW = H + E
    N = B * TB
    BIG = 65536.0
    KEY0 = BIG * E
    ROWS = T + CAP
    assert CP == P and KH * P == H == S and CAP == 2 * P and MI * P == I

    h_rows = nc.dram_tensor("h_rows", [ROWS, HW], F32, kind="Internal").ap()
    place_table = nc.dram_tensor("place_table", [CAP * E, 1], I32, kind="Internal").ap()

    with ExitStack() as ctx:
        def sem(name):
            return ctx.enter_context(nc.semaphore(name))

        def sb(name, shape, dt, where=ctx):
            return where.enter_context(nc.sbuf_tensor(name, shape, dt))

        raw_g = [sb(f"raw_g{u}", [P, KH, I], F32) for u in range(2)]
        raw_u = [sb(f"raw_u{u}", [P, KH, I], F32) for u in range(2)]
        raw_d = sb("raw_d", [P, MI, H], F32)
        ident = sb("ident", [P, P], F32)
        table = sb("table", [P, 2, E], I32)
        token_no = sb("token_no", [P, N], I32)
        where8 = [sb(f"where8_{i}", [P, TOPK], I32) for i in range(2)]

        a_mem = ExitStack()
        before = sb("before", [P, P], BF16, a_mem)
        ones = sb("ones", [P, P], BF16, a_mem)
        expert_no = sb("expert_no", [P, E], F32, a_mem)
        free_rows = sb("free_rows", [P, 2, E], I32, a_mem)
        gates = sb("gates", [P, 2], F32, a_mem)
        tanh_g = sb("tanh_g", [P, 2], F32, a_mem)
        w_qk = sb("w_qk", [P, 2, CC, D], F32, a_mem)
        b_qk = sb("b_qk", [P, 2, CC], F32, a_mem)
        gw_sb = sb("gw_sb", [P, KH, E], F32, a_mem)
        mask_u8 = raw_g[1][:].rearrange("p k i -> p (k i)").bitcast(U8)[:, 0:TB * S].rearrange("p (j s) -> p j s", j=TB)
        mask_add = sb("mask_add", [P, TB, S], BF16, a_mem)
        kpm_u8 = sb("kpm_u8", [P, S], U8, a_mem)
        kpm_add = sb("kpm_add", [P, S], BF16, a_mem)
        both_add = sb("both_add", [P, 2, S], BF16, a_mem)
        ctx_sb = [sb(f"ctx_sb{i}", [P, CC, S], F32, a_mem) for i in range(2)]
        qk = [sb(f"qk{i}", [P, 2, CC, S], F32, a_mem) for i in range(2)]
        xb = [sb(f"xb{i}", [P, H], F32, a_mem) for i in range(4)]
        junk = sb("junk", [P, S], BF16, a_mem)
        zb = [sb(f"zb{i}", [P, S], F32, a_mem) for i in range(2)]
        hT = sb("hT", [P, KH, P], F32, a_mem)
        hrow = [sb(f"hrow{i}", [P, HW], F32, a_mem) for i in range(4)]
        xsum = sb("xsum", [P, 4], F32, a_mem)
        nmean = sb("nmean", [P, 4], F32, a_mem)
        xssq = sb("xssq", [P, 4], F32, a_mem)
        sc = [sb(f"sc{i}", [P, 16], F32, a_mem) for i in range(2)]
        half_pow = sb("half_pow", [P, 2], F32, a_mem)
        norm = [sb(f"norm{i}", [P, 2], F32, a_mem) for i in range(2)]
        nbias = [sb(f"nbias{i}", [P, 1], F32, a_mem) for i in range(2)]
        psum_p = sb("psum_p", [P, 2], F32, a_mem)
        bn = [sb(f"bn{i}", [P, 2, 6], F32, a_mem) for i in range(2)]
        lg = [sb(f"lg{i}", [P, E], F32, a_mem) for i in range(2)]
        top = [sb(f"top{i}", [P, TOPK], F32, a_mem) for i in range(2)]
        ntop = [sb(f"ntop{i}", [P, 1], F32, a_mem) for i in range(2)]
        left = sb("left", [P, E], F32, a_mem)
        sel = [sb(f"sel{i}", [P, E], BF16, a_mem) for i in range(2)]
        taken = [sb(f"taken{i}", [P, E], BF16, a_mem) for i in range(2)]
        e8 = sb("e8", [P, TOPK], F32, a_mem)
        e8sum = [sb(f"e8sum{i}", [P, 1], F32, a_mem) for i in range(2)]
        ew = [sb(f"ew{i}", [P, E], F32, a_mem) for i in range(2)]
        q_ = sb("q_", [P, E], F32, a_mem)
        fits = sb("fits", [P, E], F32, a_mem)
        place = sb("place", [P, E], F32, a_mem)
        key = sb("key", [P, E], F32, a_mem)
        key8 = sb("key8", [P, TOPK], F32, a_mem)
        r8 = sb("r8", [P, 2], F32, a_mem)
        a_mem.close()

        split_g = [sb(f"split_g{u}", [P, 2, KH, I], BF16) for u in range(2)]
        split_u = [sb(f"split_u{u}", [P, 2, KH, I], BF16) for u in range(2)]
        split_d = sb("split_d", [P, 2, MI, H], BF16)
        xg = [sb(f"xg{u}", [P, 2, HW], F32) for u in range(2)]
        xT = [sb(f"xT{u}", [P, KH, 2, CAP], BF16) for u in range(2)]
        g_idx = [sb(f"g_idx{u}", [P, 2], I32) for u in range(2)]
        s_idx = [sb(f"s_idx{u}", [P, 2], I32) for u in range(2)]
        wcol = [sb(f"wcol{u}", [P, 2], F32) for u in range(2)]
        sil = sb("sil", [P, MI, CAP], F32)
        prod = sb("prod", [P, MI, CAP], F32)
        act = [sb(f"act{u}", [P, 2, MI, CAP], BF16) for u in range(2)]
        ob = [sb(f"ob{u}", [P, 2, H], F32) for u in range(2)]

        consts_made = sem("consts_made")
        small_loaded = sem("small_loaded")
        mask_loaded = sem("mask_loaded")
        tanh_ready = sem("tanh_ready")
        rows_cleared = sem("rows_cleared")
        ctx_loaded = [sem(f"ctx_loaded{i}") for i in range(2)]
        kpm_loaded = sem("kpm_loaded")
        kpm_used = sem("kpm_used")
        mask_used = sem("mask_used")
        w_loaded = sem("w_loaded")
        proj_done = sem("proj_done")
        proj_out = sem("proj_out")
        scores_done = sem("scores_done")
        scores_used = sem("scores_used")
        x_loaded = [sem(f"x_loaded{i}") for i in range(4)]
        x_summed = sem("x_summed")
        nmean_ready = sem("nmean_ready")
        x_squared = sem("x_squared")
        z_ready = sem("z_ready")
        exp_done = sem("exp_done")
        x1_ready = sem("x1_ready")
        var_ready = sem("var_ready")
        norm_ready = sem("norm_ready")
        h_done = sem("h_done")
        hT_done = sem("hT_done")
        hT_out = sem("hT_out")
        logits_done = sem("logits_done")
        chosen = sem("chosen")
        pos_done = sem("pos_done")
        ew_done = sem("ew_done")
        routed = sem("routed")
        x1_stored = [sem(f"x1_stored{i}") for i in range(4)]
        h_stored = [sem(f"h_stored{i}") for i in range(4)]
        places_stored = [sem(f"places_stored{i}") for i in range(2)]
        table_loaded = sem("table_loaded")
        dve_chain = sem("dve_chain")
        act_chain = sem("act_chain")
        pool_chain = sem("pool_chain")
        g_loaded = [sem(f"g_loaded{u}") for u in range(2)]
        u_loaded = [sem(f"u_loaded{u}") for u in range(2)]
        d_loaded = sem("d_loaded")
        g_high, g_low = sem("g_high"), sem("g_low")
        u_high, u_low = sem("u_high"), sem("u_low")
        d_high, d_low = sem("d_high"), sem("d_low")
        gathered = [sem(f"gathered{u}") for u in range(2)]
        wcol_ready = sem("wcol_ready")
        xT_done = sem("xT_done")
        xT_high = sem("xT_high")
        xT_out = sem("xT_out")
        gu_done = sem("gu_done")
        sil_done = sem("sil_done")
        act_ready = sem("act_ready")
        down_done = sem("down_done")
        down_out = sem("down_out")
        scattered = sem("scattered")

        CONSTS = 8
        SMALL = 3

        p_mem = ExitStack()
        ps = lambda name, shape, dt, where: where.enter_context(nc.psum_tensor(name, shape, dt))
        ps_s = ps("ps_s", [P, S], F32, p_mem)
        ps_t = ps("ps_t", [P, KH, P], F32, p_mem)
        ps_j = ps("ps_j", [P, NH], F32, p_mem)
        ps_l = ps("ps_l", [P, E], F32, p_mem)
        ps_p = ps("ps_p", [P, E], F32, p_mem)
        p_mem.close()
        ps_gu = [ps(f"ps_gu{m}", [P, 2, CAP], F32, ctx) for m in range(MI)]
        ps_x = [ps(f"ps_x{i}", [P, 2, CAP], F32, ctx) for i in range(2)]
        ps_d = [ps(f"ps_d{i}", [P, NH], F32, ctx) for i in range(3)]

        block = ctx.enter_context(nc.Block())

        CHUNKS = [(1, 0, 0), (1, 0, 1), (1, 1, 0), (1, 1, 1), (0, 0, 0), (0, 1, 0), (0, 0, 1), (0, 1, 1)]

        def attention_done(eng):
            eng.wait_ge(routed, N)
            for i in range(4):
                eng.wait_ge(x1_stored[i], 16 * N // 4)
                eng.wait_ge(h_stored[i], 16 * N // 4)

        @block.sync
        def _(sp):
            def load_ctx(b):
                sp.dma_start(ctx_sb[b % 2][:], ctxT[b]).then_inc(ctx_loaded[b % 2], 16)

            def load_kpm(b):
                sp.dma_start(kpm_u8[:], kpm[b].partition_broadcast(P)).then_inc(kpm_loaded, 16)

            def load_x(g):
                sp.dma_start(xb[g % 4][:], x[g * P:(g + 1) * P, :]).then_inc(x_loaded[g % 4], 16)

            def load_expert(e, u):
                sp.dma_start(raw_g[u][:], wg[bass.ds(e, 1)].rearrange("e p k i -> p (e k) i")).then_inc(g_loaded[u], 16)
                sp.dma_start(raw_u[u][:], wu[bass.ds(e, 1)].rearrange("e p k i -> p (e k) i")).then_inc(u_loaded[u], 16)

            def load_down(e):
                sp.dma_start(raw_d[:], wd[bass.ds(e, 1)].rearrange("e p m h -> p (e m) h")).then_inc(d_loaded, 16)

            def store_h(g):
                sp.wait_ge(routed, g + 1)
                sp.dma_start(h_rows[g * P:(g + 1) * P, :], hrow[g % 4][:]).then_inc(h_stored[g % 4], 16)

            sp.dma_start(w_qk[:, 1], wkT).then_inc(w_loaded, 16)
            sp.dma_start(b_qk[:, 1], bkT).then_inc(w_loaded, 16)
            load_ctx(0)
            sp.dma_start(w_qk[:, 0], wqT).then_inc(w_loaded, 16)
            sp.dma_start(b_qk[:, 0], bqT).then_inc(w_loaded, 16)
            load_x(0)
            sp.dma_start(gates[:, 0:1], g_x.partition_broadcast(P)).then_inc(small_loaded, 16)
            sp.dma_start(gates[:, 1:2], g_f.partition_broadcast(P)).then_inc(small_loaded, 16)
            load_kpm(0)
            sp.dma_start(mask_u8, mask.rearrange("(j p) s -> p j s", p=P)).then_inc(mask_loaded, 16)
            load_x(1)
            sp.dma_start(gw_sb[:], gwT).then_inc(small_loaded, 16)
            load_x(2)
            load_x(3)
            load_ctx(1)
            sp.wait_ge(consts_made, CONSTS)
            for half in range(2):
                r = slice(T + half * P, T + (half + 1) * P)
                sp.dma_start(h_rows[r, :], hrow[3][:]).then_inc(rows_cleared, 16)
                sp.dma_start(out[r, :], hrow[3][:, 0:H]).then_inc(rows_cleared, 16)
            sp.dma_start(place_table.rearrange("(p k) o -> p (k o)", p=P),
                         free_rows[:].rearrange("p t e -> p (t e)")).then_inc(rows_cleared, 16)

            for g in range(N):
                b, j = g // TB, g % TB
                sp.wait_ge(x1_ready, g + 1)
                sp.dma_start(out[g * P:(g + 1) * P, :], xb[g % 4][:]).then_inc(x1_stored[g % 4], 16)
                if g >= 2:
                    store_h(g - 2)
                if 1 <= g < N - 3:
                    sp.wait_ge(x1_stored[(g - 1) % 4], 16 * ((g - 1) // 4 + 1))
                    sp.wait_ge(h_done, g)
                    load_x(g + 3)
                if g == TB:
                    load_expert(0, 0)
                if g == TB + 2:
                    load_down(0)
                if g == TB + 4:
                    sp.wait_ge(mask_used, TB)
                    load_expert(1, 1)
                if j == 0 and b < B - 2:
                    sp.wait_ge(proj_done, 8 * (b + 1))
                    load_ctx(b + 2)
                if j == 0 and b < B - 1:
                    sp.wait_ge(kpm_used, b + 1)
                    load_kpm(b + 1)
            for g in (N - 2, N - 1):
                store_h(g)
            for i in range(2):
                sp.wait_ge(places_stored[i], 16 * TOPK * N // 2)
            sp.dma_start(table[:].rearrange("p t e -> p (t e)"),
                         place_table.rearrange("(p k) o -> p (k o)", p=P)).then_inc(table_loaded, 16)

            def expert(e, u, ahead):
                if ahead >= 1:
                    sp.wait_ge(d_low, 2 * e + 2)
                    load_down(e + 1)
                if ahead >= 2:
                    sp.wait_ge(g_low, 2 * e + 2)
                    sp.wait_ge(u_low, 2 * e + 2)
                    load_expert(e + 2, u)

            with sp.Fori(0, E // 2 - 1) as i:
                expert(2 * i, 0, 2)
                expert(2 * i + 1, 1, 2)
            expert(E - 2, 0, 1)
            sp.wait_ge(scattered, 32 * E)

        @block.tensor
        def _(pe):
            def project(b, i):
                which, o, n = CHUNKS[i]
                bank = ps_t[:, 0:NH // P].rearrange("p k t -> p (k t)") if b == 0 and i % 2 else ps_j[:]
                pe.wait_ge(ctx_loaded[b % 2], 16 * (b // 2 + 1))
                behind = 8 * b + i - (1 if b == 0 else 0)
                if behind > 0:
                    pe.wait_ge(proj_out, behind)
                for k in range(CC):
                    mm = pe.matmul(bank, w_qk[:, which, k, o * P:(o + 1) * P], ctx_sb[b % 2][:, k, n * NH:(n + 1) * NH],
                                   start=(k == 0), stop=(k == CC - 1))
                mm.then_inc(proj_done, 1)

            def scores(g):
                b, j = g // TB, g % TB
                pe.wait_ge(proj_out, 8 * b + (6 if j < TB // 2 else 8))
                if g:
                    pe.wait_ge(scores_used, g)
                for n in range(S // NH):
                    for k in range(CC):
                        mm = pe.matmul(ps_s[:, n * NH:(n + 1) * NH], qk[b % 2][:, 0, k, j * P:(j + 1) * P],
                                       qk[b % 2][:, 1, k, n * NH:(n + 1) * NH], start=(k == 0), stop=(k == CC - 1))
                mm.then_inc(scores_done, 1)

            def turn_h(g):
                pe.wait_ge(h_done, g + 1)
                if g:
                    pe.wait_ge(hT_out, g)
                for k in range(KH):
                    mm = pe.transpose(ps_t[:, k, :], hrow[g % 4][:, k * P:(k + 1) * P], ident[:])
                mm.then_inc(hT_done, 1)

            def logits(g):
                pe.wait_ge(hT_out, g + 1)
                if g:
                    pe.wait_ge(chosen, g)
                for k in range(KH):
                    mm = pe.matmul(ps_l[:], hT[:, k, :], gw_sb[:, k, :], start=(k == 0), stop=(k == KH - 1))
                mm.then_inc(logits_done, 1)

            def positions(g):
                pe.wait_ge(chosen, g + 1)
                if g:
                    pe.wait_ge(routed, g)
                pe.matmul(ps_p[:], before[:], sel[g % 2][:], start=True, stop=False)
                pe.matmul(ps_p[:], ones[:], taken[g % 2][:], start=False, stop=True).then_inc(pos_done, 1)

            pe.wait_ge(w_loaded, 16 * 4)
            for i in range(6):
                project(0, i)
            scores(0)
            project(0, 6)
            scores(1)
            project(0, 7)
            pe.wait_ge(small_loaded, 16 * SMALL)
            pe.wait_ge(consts_made, CONSTS)
            for g in range(N + 1):
                if g >= 1:
                    logits(g - 1)
                if g + 2 < N:
                    scores(g + 2)
                if g >= 1:
                    positions(g - 1)
                if g < N:
                    turn_h(g)
                if g + TB < N:
                    project(g // TB + 1, g % TB)

            def turn(e, u, q, first=False):
                pe.wait_ge(gathered[u], 16 * (e - u) + 32)
                if not (first and q < 2):
                    pe.wait_ge(xT_out, 4 * e + q - 1)
                for kk in range(2):
                    for half in range(2):
                        at = (2 * q + kk) * P
                        mm = pe.transpose(ps_x[q % 2][:, kk, half * P:(half + 1) * P], xg[u][:, half, at:at + P], ident[:])
                mm.then_inc(xT_done, 1)

            PAIRS = ((0, 0), (0, 1), (1, 0))

            def gate_up(e, u, m, first=False):
                if not first:
                    pe.wait_ge(act_ready, MI * e - MI + m + 1)
                for t, w in ((0, split_g[u]), (1, split_u[u])):
                    if m == 0:
                        pe.wait_ge((g_low, u_low)[t], 2 * e + 2)
                    for k in range(KH):
                        if m == 0 and t == 0 and k % 2 == 0:
                            pe.wait_ge(xT_out, 4 * e + k // 2 + 1)
                        for wi, xi in PAIRS:
                            mm = pe.matmul(ps_gu[m][:, t, :], w[:, wi, k, m * P:(m + 1) * P], xT[u][:, k, xi, :],
                                           start=(k == 0 and (wi, xi) == (0, 0)),
                                           stop=(k == KH - 1 and (wi, xi) == (1, 0)))
                mm.then_inc(gu_done, 1)

            def down_part(u, n, ms):
                half, c = n // 2, n % 2
                for m in ms:
                    for wi, ai in PAIRS:
                        mm = pe.matmul(ps_d[n % 3][:], act[u][:, ai, m, half * P:(half + 1) * P],
                                       split_d[:, wi, m, c * NH:(c + 1) * NH],
                                       start=(m == 0 and (wi, ai) == (0, 0)),
                                       stop=(m == MI - 1 and (wi, ai) == (1, 0)))
                return mm

            def down(e, u, first=False):
                pe.wait_ge(d_low, 2 * e + 2)
                pe.wait_ge(act_ready, MI * e + MI - 1)
                for n in range(2):
                    if not first:
                        pe.wait_ge(down_out, 4 * e - 2 * n)
                    down_part(u, n, range(MI - 1))
                pe.wait_ge(act_ready, MI * e + MI)
                for n in range(2):
                    down_part(u, n, [MI - 1]).then_inc(down_done, 1)
                if not first:
                    pe.wait_ge(down_out, 4 * e - 1)
                down_part(u, 2, range(MI)).then_inc(down_done, 1)
                pe.wait_ge(down_out, 4 * e + 1)
                down_part(u, 3, range(MI)).then_inc(down_done, 1)

            def expert(e, u, first=False, last=False):
                for m in range(MI):
                    gate_up(e, u, m, first)
                    if m < 2 and not last:
                        turn(e + 1, 1 - u, 2 * m)
                        turn(e + 1, 1 - u, 2 * m + 1)
                down(e, u, first)

            attention_done(pe)
            for q in range(4):
                turn(0, 0, q, True)
            expert(0, 0, True)
            with pe.Fori(0, E // 2 - 1) as i:
                expert(2 * i + 1, 1)
                expert(2 * i + 2, 0)
            expert(E - 1, 1, False, True)

        @block.scalar
        def _(s):
            chain = Chain(s, act_chain)
            s.wait_ge(w_loaded, 16 * 4)

            def project_out(b, i):
                which, o, n = CHUNKS[i]
                bank = ps_t[:, 0:NH // P].rearrange("p k t -> p (k t)") if b == 0 and i % 2 else ps_j[:]
                s.wait_ge(proj_done, 8 * b + i + 1)
                if b >= 2 and i == 0:
                    s.wait_ge(scores_done, (b - 1) * TB)
                s.activation(qk[b % 2][:, which, o, n * NH:(n + 1) * NH], bank, ACT.Identity,
                             bias=b_qk[:, which, o:o + 1]).then_inc(proj_out, 1)

            def x_sum(g):
                s.wait_ge(x_loaded[g % 4], 16 * (g // 4 + 1))
                if g == 1:
                    s.wait_ge(x_summed, 1)
                if g >= 2:
                    s.wait_ge(x_squared, g)
                s.activation(junk[:], xb[g % 4][:], ACT.Identity, accum_out=xsum[:, g % 4:g % 4 + 1]).then_inc(x_summed, 1)

            def x_square(g):
                s.wait_ge(nmean_ready, g + 1)
                s.wait_ge(x_summed, max(g + 1, 2))
                s.activation(junk[:], xb[g % 4][:], ACT.Square, bias=nmean[:, g % 4:g % 4 + 1],
                             accum_out=xssq[:, g % 4:g % 4 + 1]).then_inc(x_squared, 1)

            def softmax(g):
                s.wait_ge(z_ready, g + 1)
                s.activation(zb[g % 2][:], zb[g % 2][:], ACT.Exp, bias=sc[g % 2][:, 2:3], scale=norm[1 - g % 2][:, 1:2],
                             accum_out=psum_p[:, g % 2:g % 2 + 1]).then_inc(exp_done, 1)

            def normalize(g):
                s.wait_ge(norm_ready, g + 2)
                if g >= 2:
                    s.wait_ge(h_done, g - 1)
                chain.link(s.activation(nbias[g % 2][:], sc[g % 2][:, 9:10], ACT.Copy, scale=norm[g % 2][:, 0:1]))
                if g == 3:
                    s.wait_ge(rows_cleared, 16 * 5)
                if g >= 4:
                    s.wait_ge(h_stored[g % 4], 16 * (g // 4))
                s.activation(hrow[g % 4][:, 0:H], xb[g % 4][:], ACT.Identity, bias=nbias[g % 2][:],
                             scale=norm[g % 2][:, 0:1]).then_inc(h_done, 1)

            def turned_out(g):
                s.wait_ge(hT_done, g + 1)
                if g:
                    s.wait_ge(logits_done, g)
                s.activation(hT[:], ps_t[:], ACT.Copy).then_inc(hT_out, 1)

            def expert_weights(g):
                u = g % 2
                s.wait_ge(chosen, g + 1)
                if g:
                    s.wait_ge(ew_done, g)
                s.activation(e8[:], top[u][:], ACT.Exp, bias=ntop[u][:], accum_out=e8sum[u][:])
                s.activation(ew[u][:], lg[u][:], ACT.Exp, bias=ntop[u][:]).then_inc(ew_done, 1)

            for i in range(6):
                project_out(0, i)
            x_sum(0)
            x_sum(1)
            x_square(0)
            s.wait_ge(small_loaded, 16 * SMALL)
            s.activation(tanh_g[:], gates[:], ACT.Tanh).then_inc(tanh_ready, 1)
            project_out(0, 6)
            for g in range(N + 1):
                if g < N:
                    softmax(g)
                if g == 0:
                    project_out(0, 7)
                if g >= 1:
                    turned_out(g - 1)
                    if g - 1 + TB < N:
                        project_out((g - 1) // TB + 1, (g - 1) % TB)
                if g + 1 < N:
                    x_square(g + 1)
                if g + 2 < N:
                    x_sum(g + 2)
                if g < N:
                    normalize(g)
                if g >= 1:
                    expert_weights(g - 1)

            attention_done(s)

            def gate_high(e, u, part, first=False):
                s.wait_ge(g_loaded[u], 8 * (e - u) + 16)
                if not first:
                    s.wait_ge(gu_done, MI * e - MI)
                ks = slice(part * KH // 2, (part + 1) * KH // 2)
                s.activation(split_g[u][:, 0, ks], raw_g[u][:, ks], ACT.Copy).then_inc(g_high, 1)

            def up_high(e, u, part, first=False):
                s.wait_ge(u_loaded[u], 8 * (e - u) + 16)
                if not first:
                    s.wait_ge(gu_done, MI * e - MI)
                ks = slice(part * KH // 2, (part + 1) * KH // 2)
                s.activation(split_u[u][:, 0, ks], raw_u[u][:, ks], ACT.Copy).then_inc(u_high, 1)

            def down_high(e, part, first=False):
                s.wait_ge(d_loaded, 16 * e + 16)
                if not first:
                    s.wait_ge(down_done, 4 * e)
                cs = slice(part * NH, (part + 1) * NH)
                s.activation(split_d[:, 0, :, cs], raw_d[:, :, cs], ACT.Copy).then_inc(d_high, 1)

            def silu(e, m):
                s.wait_ge(gu_done, MI * e + m + 1)
                s.activation(sil[:, m], ps_gu[m][:, 0], ACT.Silu).then_inc(sil_done, 1)

            def turned_high(e, u, q):
                s.wait_ge(xT_done, 4 * e + q + 1)
                s.activation(xT[u][:, 2 * q:2 * q + 2, 0], ps_x[q % 2][:], ACT.Copy).then_inc(xT_high, 1)

            def rows_out(e, u, first=False):
                s.wait_ge(wcol_ready, e + 1)
                if not first:
                    s.wait_ge(scattered, 32 * e - 32)
                for n in range(4):
                    s.wait_ge(down_done, 4 * e + n + 1)
                    s.activation(ob[u][:, n // 2, n % 2 * NH:(n % 2 + 1) * NH], ps_d[n % 3][:], ACT.Copy,
                                 scale=wcol[u][:, n // 2:n // 2 + 1]).then_inc(down_out, 1)

            def expert(e, u, first=False, last=False):
                none_before = first and u == 0
                down_high(e, 0, none_before)
                down_high(e, 1, none_before)
                silu(e, 0)
                if not last:
                    turned_high(e + 1, 1 - u, 0)
                    turned_high(e + 1, 1 - u, 1)
                    gate_high(e + 1, 1 - u, 0, none_before)
                    gate_high(e + 1, 1 - u, 1, none_before)
                silu(e, 1)
                if not last:
                    turned_high(e + 1, 1 - u, 2)
                    turned_high(e + 1, 1 - u, 3)
                    up_high(e + 1, 1 - u, 0, none_before)
                silu(e, 2)
                if not last:
                    up_high(e + 1, 1 - u, 1, none_before)
                rows_out(e, u, first)

            for part in range(2):
                gate_high(0, 0, part, True)
            for part in range(2):
                up_high(0, 0, part, True)
            for q in range(4):
                turned_high(0, 0, q)
            expert(0, 0, True)
            expert(1, 1, True)
            with s.Fori(1, E // 2 - 1) as i:
                expert(2 * i, 0)
                expert(2 * i + 1, 1)
            expert(E - 2, 0)
            expert(E - 1, 1, False, True)

        @block.vector
        def _(v):
            chain = Chain(v, dve_chain)

            def minus_mean(g):
                v.wait_ge(x_summed, g + 1)
                v.tensor_scalar(nmean[:, g % 4:g % 4 + 1], xsum[:, g % 4:g % 4 + 1], -1.0 / H, None,
                                ALU.mult).then_inc(nmean_ready, 1)

            def x_variance(g):
                v.wait_ge(x_squared, g + 1)
                return v.tensor_scalar(sc[1 - g % 2][:, 7:8], xssq[:, g % 4:g % 4 + 1], D / H, D * LN_EPS, ALU.mult, ALU.add)

            def scaled_scores(g):
                v.wait_ge(nmean_ready, g + 1)
                v.wait_ge(scores_done, g + 1)
                v.scalar_tensor_tensor(zb[g % 2][:], xb[g % 4][:], nmean[:, g % 4:g % 4 + 1], ps_s[:], ALU.add,
                                       ALU.mult).then_inc(scores_used, 1)

            def key_mask(b):
                v.wait_ge(kpm_loaded, 16 * (b + 1))
                v.tensor_scalar(kpm_add[:], kpm_u8[:], MASKED, None, ALU.mult).then_inc(kpm_used, 1)

            def both(g):
                v.wait_ge(kpm_used, g // TB + 1)
                return chain.mark(v.tensor_tensor(both_add[:, g % 2], mask_add[:, g % TB], kpm_add[:], ALU.add))

            def route(g):
                u = g % 2
                v.wait_ge(pos_done, g + 1)
                t = chain.mark(v.scalar_tensor_tensor(q_[:], sel[u][:], -BIG, ps_p[:], ALU.mult, ALU.add))
                yield
                chain.wait(t)
                v.tensor_scalar(fits[:], q_[:], CAP - BIG, None, ALU.is_lt)
                t = chain.mark(v.scalar_tensor_tensor(place[:], q_[:], float(E), expert_no[:], ALU.mult, ALU.add))
                yield
                chain.wait(t)
                t = chain.mark(v.scalar_tensor_tensor(key[:], place[:], -1.0, fits[:], ALU.mult, ALU.mult))
                v.wait_ge(ew_done, g + 1)
                r = chain.mark(v.reciprocal(r8[:, 0:1], e8sum[u][:]))
                yield
                chain.wait(t)
                t = chain.mark(v.max(key8[:], key[:]))
                chain.wait(r)
                r = chain.mark(v.tensor_tensor(r8[:, 1:2], r8[:, 0:1], tanh_g[:, 1:2], ALU.mult))
                yield
                if g >= 2:
                    v.wait_ge(places_stored[u], 16 * TOPK * (g // 2))
                chain.wait(r)
                chain.mark(v.tensor_scalar(where8[u][:], key8[:], -1.0, KEY0, ALU.mult, ALU.add))
                v.scalar_tensor_tensor(hrow[g % 4][:, H:HW], ew[u][:], r8[:, 1:2], fits[:], ALU.mult,
                                       ALU.mult).then_inc(routed, 1)
                yield

            def choose(g):
                u = g % 2
                v.wait_ge(logits_done, g + 1)
                if g >= 2:
                    v.wait_ge(ew_done, g - 1)
                t = chain.mark(v.tensor_copy(lg[u][:], ps_l[:]))
                yield
                chain.wait(t)
                t = chain.mark(v.max(top[u][:], lg[u][:]))
                yield
                chain.wait(t)
                t = chain.mark(v.match_replace(left[:], top[u][:], lg[u][:], -3.0e38))
                v.tensor_scalar(ntop[u][:], top[u][:, 0:1], -1.0, None, ALU.mult)
                yield
                chain.wait(t)
                if g >= 1:
                    v.wait_ge(pos_done, g)
                t = chain.mark(v.tensor_scalar(sel[u][:], left[:], -3.0e38, None, ALU.is_le))
                yield
                chain.wait(t)
                v.tensor_tensor(taken[1 - u][:], taken[u][:], sel[u][:], ALU.add).then_inc(chosen, 1)
                yield

            v.wait_ge(mask_loaded, 16)
            for j in range(TB):
                v.tensor_scalar(mask_add[:, j], mask_u8[:, j], MASKED, None, ALU.mult).then_inc(mask_used, 1)
            chain.mark(v.memset(taken[0][:], 0.0))
            key_mask(0)
            v.wait_ge(mask_used, TB)
            both_made = both(0)
            minus_mean(0)
            minus_mean(1)
            x_variance(0).then_inc(var_ready, 1)
            v.wait_ge(consts_made, CONSTS)
            scaled_scores(0)
            v.wait_ge(tanh_ready, 1)
            for g in range(N):
                u, f = g % 2, g % 4
                c = sc[u]
                places = route(g - 2) if g >= 2 else iter(())
                older = choose(g - 1) if g >= 1 else iter(())
                v.wait_ge(scores_used, g + 1)
                chain.wait(both_made)
                t = chain.mark(v.tensor_tensor_reduce(zb[u][:], zb[u][:], both_add[:, u], 1.0, -3.0e38, ALU.add,
                                                      ALU.max, c[:, 3:4]))
                v.wait_ge(norm_ready, g + 1)
                chain.wait(t)
                v.scalar_tensor_tensor(c[:, 2:3], c[:, 3:4], -1.0, norm[1 - u][:, 1:2], ALU.mult, ALU.mult
                                       ).then_inc(z_ready, 1)
                if g + 1 < N:
                    scaled_scores(g + 1)
                v.wait_ge(exp_done, g + 1)
                t = chain.mark(v.reciprocal(c[:, 4:5], psum_p[:, u:u + 1]))
                next(places, None)
                chain.wait(t)
                t = chain.mark(v.tensor_tensor(c[:, 5:6], c[:, 4:5], tanh_g[:, 0:1], ALU.mult))
                next(places, None)
                chain.wait(t)
                v.wait_ge(x_squared, g + 1)
                v.scalar_tensor_tensor(xb[f][:], zb[u][:], c[:, 5:6], xb[f][:], ALU.mult, ALU.add).then_inc(x1_ready, 1)
                next(places, None)
                v.wait_ge(x1_ready, g + 1)
                v.bn_stats(bn[u][:, 0], xb[f][:, 0:NH])
                next(places, None)
                t = chain.mark(v.bn_stats(bn[u][:, 1], xb[f][:, NH:2 * NH]))
                next(places, None)
                chain.wait(t)
                t = chain.mark(v.bn_aggr(c[:, 10:12], bn[u][:].rearrange("p a b -> p (a b)")))
                next(older, None)
                chain.wait(t)
                if g >= 2:
                    v.wait_ge(norm_ready, g)
                    v.wait_ge(h_done, g - 1)
                v.tensor_scalar(c[:, 9:10], c[:, 10:11], -1.0, None, ALU.mult)
                if g + 1 < N:
                    x_variance(g + 1)
                v.tensor_scalar(c[:, 6:7], c[:, 11:12], LN_EPS, None, ALU.add).then_inc(var_ready, 1)
                for _ in older:
                    pass
                if g + 1 < N:
                    if (g + 1) % TB == 0:
                        key_mask((g + 1) // TB)
                    both_made = both(g + 1)
                if g + 2 < N:
                    minus_mean(g + 2)
            for steps in (route(N - 2), choose(N - 1), route(N - 1)):
                for _ in steps:
                    pass

            attention_done(v)

            def gate_low(e, u, part):
                v.wait_ge(g_high, 2 * e + part + 1)
                ks = slice(part * KH // 2, (part + 1) * KH // 2)
                v.tensor_tensor(split_g[u][:, 1, ks], raw_g[u][:, ks], split_g[u][:, 0, ks], ALU.subtract).then_inc(g_low, 1)

            def up_low(e, u, part):
                v.wait_ge(u_high, 2 * e + part + 1)
                ks = slice(part * KH // 2, (part + 1) * KH // 2)
                v.tensor_tensor(split_u[u][:, 1, ks], raw_u[u][:, ks], split_u[u][:, 0, ks], ALU.subtract).then_inc(u_low, 1)

            def down_low(e, part):
                v.wait_ge(d_high, 2 * e + part + 1)
                cs = slice(part * NH, (part + 1) * NH)
                v.tensor_tensor(split_d[:, 1, :, cs], raw_d[:, :, cs], split_d[:, 0, :, cs], ALU.subtract
                                ).then_inc(d_low, 1)

            def activate(e, u, m, first):
                v.wait_ge(sil_done, MI * e + m + 1)
                if m == 0 and not first:
                    v.wait_ge(down_done, 4 * e - 4)
                chain.link(v.tensor_tensor(prod[:, m], sil[:, m], ps_gu[m][:, 1], ALU.mult))
                chain.link(v.tensor_copy(act[u][:, 0, m], prod[:, m]))
                v.tensor_tensor(act[u][:, 1, m], prod[:, m], act[u][:, 0, m], ALU.subtract).then_inc(act_ready, 1)

            def turned_low(e, u, q):
                v.wait_ge(xT_high, 4 * e + q + 1)
                v.tensor_tensor(xT[u][:, 2 * q:2 * q + 2, 1], ps_x[q % 2][:], xT[u][:, 2 * q:2 * q + 2, 0], ALU.subtract
                                ).then_inc(xT_out, 1)

            def expert(e, u, first=False, last=False):
                down_low(e, 0)
                down_low(e, 1)
                activate(e, u, 0, first)
                if not last:
                    turned_low(e + 1, 1 - u, 0)
                    turned_low(e + 1, 1 - u, 1)
                    gate_low(e + 1, 1 - u, 0)
                    gate_low(e + 1, 1 - u, 1)
                activate(e, u, 1, first)
                if not last:
                    turned_low(e + 1, 1 - u, 2)
                    turned_low(e + 1, 1 - u, 3)
                    up_low(e + 1, 1 - u, 0)
                activate(e, u, 2, first)
                if not last:
                    up_low(e + 1, 1 - u, 1)

            for part in range(2):
                gate_low(0, 0, part)
            for part in range(2):
                up_low(0, 0, part)
            for q in range(4):
                turned_low(0, 0, q)
            expert(0, 0, True)
            expert(1, 1, True)
            with v.Fori(1, E // 2 - 1) as i:
                chain.enter(i - 1, 12)
                expert(2 * i, 0)
                expert(2 * i + 1, 1)
                chain.leave(E // 2 - 2, 12)
            expert(E - 2, 0)
            expert(E - 1, 1, False, True)

        @block.gpsimd
        def _(p):
            chain = Chain(p, pool_chain)
            p.memset(ones[:], 1.0).then_inc(consts_made, 1)
            p.memset(half_pow[:], -0.5).then_inc(consts_made, 1)
            p.memset(ident[:], 0.0)
            made = chain.mark(p.memset(before[:], 1.0))
            p.memset(hrow[3][:], 0.0).then_inc(consts_made, 1)
            p.iota(free_rows[:], pattern=[[1, 2], [0, E]], base=T, channel_multiplier=2).then_inc(consts_made, 1)
            p.iota(token_no[:], pattern=[[P, N]], base=0, channel_multiplier=1).then_inc(consts_made, 1)
            p.iota(expert_no[:], pattern=[[1, E]], base=0, channel_multiplier=0,
                   allow_small_or_imprecise_dtypes=True).then_inc(consts_made, 1)
            chain.wait(made)
            p.affine_select(out=ident[:], in_=ident[:], compare_op=ALU.not_equal, fill=1.0, base=0,
                            pattern=[[-1, P]], channel_multiplier=1).then_inc(consts_made, 1)
            p.affine_select(out=before[:], in_=before[:], compare_op=ALU.is_gt, fill=0.0, base=0,
                            pattern=[[1, P]], channel_multiplier=-1).then_inc(consts_made, 1)

            def x1_norm(g):
                u = g % 2
                p.wait_ge(var_ready, g + 2)
                if g >= 2:
                    p.wait_ge(h_done, g - 1)
                n = 2 if g + 1 < N else 1
                p.tensor_tensor(norm[u][:, 0:n], sc[u][:, 6:6 + n], half_pow[:, 0:n], ALU.pow).then_inc(norm_ready, 1)

            def scatter_places(g):
                u = g % 2
                p.wait_ge(routed, g + 1)
                for k in range(TOPK):
                    p.indirect_dma_start(
                        out=place_table, out_offset=bass.IndirectOffsetOnAxis(ap=where8[u][:, k:k + 1].bitcast(U32), axis=0),
                        in_=token_no[:, g:g + 1], in_offset=None, bounds_check=CAP * E - 1, oob_is_err=False,
                    ).then_inc(places_stored[u], 16)

            p.wait_ge(consts_made, CONSTS)
            p.wait_ge(var_ready, 1)
            p.tensor_tensor(norm[1][:, 1:2], sc[1][:, 7:8], half_pow[:, 0:1], ALU.pow).then_inc(norm_ready, 1)
            p.wait_ge(rows_cleared, 16 * 5)
            for g in range(N + 2):
                if g < N:
                    x1_norm(g)
                if g >= 2:
                    scatter_places(g - 2)

            attention_done(p)
            for i in range(2):
                p.wait_ge(places_stored[i], 16 * TOPK * N // 2)
            p.wait_ge(table_loaded, 16)

            last_row = p.alloc_register("last_row")
            p.reg_mov(last_row, ROWS - 1)

            def hold():
                p.reg_alu(last_row, last_row, ROWS - 1, op=ALU.min)

            def gather(e, u):
                chain.link(p.tensor_copy(g_idx[u][:], table[:, :, bass.ds(e, 1)].rearrange("p t e -> p (t e)")))
                hold()
                for half in range(2):
                    p.indirect_dma_start(
                        out=xg[u][:, half, :], out_offset=None, in_=h_rows,
                        in_offset=bass.IndirectOffsetOnAxis(ap=g_idx[u][:, half:half + 1].bitcast(U32), axis=0),
                        bounds_check=last_row, oob_is_err=True,
                    ).then_inc(gathered[u], 16)

            def weights(e, u, first=False):
                p.wait_ge(gathered[u], 16 * (e - u) + 32)
                if not first:
                    p.wait_ge(down_out, 4 * e - 4)
                    p.wait_ge(scattered, 32 * e - 32)
                p.tensor_copy(wcol[u][:], xg[u][:, :, bass.ds(e + H, 1)].rearrange("p t e -> p (t e)")
                              ).then_inc(wcol_ready, 1)
                chain.link(p.tensor_copy(s_idx[u][:], g_idx[u][:]))

            def add_rows(e, u, first=False):
                if not first:
                    p.wait_ge(scattered, 32 * e)
                for half in range(2):
                    p.wait_ge(down_out, 4 * e + 2 * half + 2)
                    hold()
                    p.indirect_dma_start(
                        out=out, out_offset=bass.IndirectOffsetOnAxis(ap=s_idx[u][:, half:half + 1].bitcast(U32), axis=0),
                        in_=ob[u][:, half, :], in_offset=None, bounds_check=last_row, oob_is_err=True,
                        compute_op=ALU.add,
                    ).then_inc(scattered, 16)

            def expert(e, u, first=0, ahead=2):
                if ahead >= 2:
                    p.wait_ge(xT_done, 4 * e + 4)
                    p.wait_ge(wcol_ready, e + 1)
                    gather(e + 2, u)
                if ahead >= 1:
                    weights(e + 1, 1 - u, first == 1)
                add_rows(e, u, first == 1)

            gather(0, 0)
            gather(1, 1)
            weights(0, 0, True)
            expert(0, 0, 1)
            expert(1, 1)
            with p.Fori(1, E // 2 - 1) as i:
                chain.enter(i - 1, 4)
                expert(2 * i, 0)
                expert(2 * i + 1, 1)
                chain.leave(E // 2 - 2, 4)
            expert(E - 2, 0, 0, 1)
            expert(E - 1, 1, 0, 0)


def kernel(**inputs):
    import concourse.bacc as bacc
    from concourse.bass_utils import run_bass_kernel_spmd

    a = {k: np.asarray(v) for k, v in inputs.items()}
    B, S, H = a["x"].shape
    E, _, I = a["L0_ffn_wg"].shape
    D = a["ctx_512"].shape[2]

    def tiles(w, axis):
        shape = w.shape[:axis] + (w.shape[axis] // P, P) + w.shape[axis + 1:]
        return w.reshape(shape).swapaxes(axis, axis + 1)

    arrays = {
        "x": a["x"].reshape(B * S, H),
        "ctxT": tiles(a["ctx_512"].transpose(0, 2, 1), 1),
        "mask": a["mask_SxS2_bk1"],
        "kpm": a["mask_BxS2_bf0"],
        "g_x": a["g_xattn"], "g_f": a["g_ffn"],
        "wqT": tiles(a["L0_xattn_Wq"].T, 0), "bqT": tiles(a["L0_xattn_bq"], 0),
        "wkT": tiles(a["L0_xattn_Wk"].T, 0), "bkT": tiles(a["L0_xattn_bk"], 0),
        "gwT": tiles(a["L0_ffn_gate_w"].T, 0),
        "wg": tiles(a["L0_ffn_wg"], 1), "wu": tiles(a["L0_ffn_wu"], 1), "wd": tiles(a["L0_ffn_wd"], 1),
    }
    nc = bacc.Bacc("TRN2", target_bir_lowering=False, num_devices=1)
    sent, aps = {}, []
    for name, v in arrays.items():
        v = np.ascontiguousarray(v)
        sent[f"in_{name}"] = v
        aps.append(nc.dram_tensor(f"in_{name}", v.shape, mybir.dt.from_np(v.dtype), kind="ExternalInput").ap())
    out = nc.dram_tensor("out", (B * S + CAP, H), F32, kind="ExternalOutput").ap()
    flamingo_moe(nc, *aps, out)
    r = run_bass_kernel_spmd(nc, [sent], core_ids=[0])
    return r.results[0]["out"][:B * S].reshape(B, S, H)
```
